# Optimizing a Trainium2 kernel written in Bass

```python
import numpy as np
import jax
import jax.numpy as jnp

def _softmax(x, axis=-1):
    return jax.nn.softmax(x, axis=axis)

def _gelu(x):
    return jax.nn.gelu(x, approximate=True)

def _silu(x):
    return jax.nn.silu(x)

def _sigmoid(x):
    return jax.nn.sigmoid(x)

def _layernorm(x, axis=-1, eps=1e-05):
    m = jnp.mean(x, axis=axis, keepdims=True)
    v = jnp.var(x, axis=axis, keepdims=True)
    return (x - m) / jnp.sqrt(v + eps)

def _scatter_add(tgt, idx, src, axis=0):
    return tgt.at[idx].add(src)

def _segment_sum(src, seg, n):
    return jax.ops.segment_sum(src, seg, n)
kernel_name = 'mk_xattn_ffn_d1_seqx_r4_213fec'

def setup_inputs(seed: int=0):
    np.random.seed(seed)
    _w = jnp.asarray

    def _rec_inputs():
        import jax
        import jax.numpy as jnp
        _rk = jax.random.key(seed)
        x = -0.000125 + 0.9999 * jax.random.normal(jax.random.fold_in(_rk, 1), (4, 512, 512), jnp.float32)
        _lenS = 512 - jax.random.randint(jax.random.fold_in(_rk, 7), (4,), 0, max(1, 512 // 4) + 1, jnp.int32)
        _lenS2 = 512 - jax.random.randint(jax.random.fold_in(_rk, 8), (4,), 0, max(1, 512 // 4) + 1, jnp.int32)
        itok_BxS_13_99985 = jax.random.randint(jax.random.fold_in(_rk, 11), (4, 512), 13, 99986, jnp.int32)
        _ctx_2048P = jax.random.normal(jax.random.fold_in(_rk, 12), (4, 16, 512), jnp.float32)
        _ctx_2048c = jax.random.dirichlet(jax.random.fold_in(_rk, 512), 0.3 * jnp.ones((16,), jnp.float32), (4, 512))
        _ctx_2048t = jnp.einsum('bsk,bkd->bsd', _ctx_2048c, _ctx_2048P)
        _ctx_2048t = _ctx_2048t * jax.lax.rsqrt(jnp.mean(jnp.square(_ctx_2048t)) + 1e-12) * 0.953939
        ctx_2048 = 6.82029e-06 + 0.0200006 * (_ctx_2048t + 0.3 * jax.random.normal(jax.random.fold_in(_rk, 612), (4, 512, 512), jnp.float32))
        return (x, itok_BxS_13_99985, ctx_2048)
    x, itok_BxS_13_99985, ctx_2048 = _rec_inputs()

    def _L0_xattn_setup():
        import jax, jax.numpy as jnp
        import numpy as np
        B, S, D = (4, 1024, 512)
        E = 4
        F = 2048 // E
        VOCAB = 25000
        key = jax.random.key(seed)
        k1, k2, k3, k4, k5 = jax.random.split(key, 5)
        hidden_states = jax.random.normal(k1, (B, S, D), dtype=jnp.float32)
        token_ids = jax.random.randint(k2, (B, S), 0, VOCAB, dtype=jnp.int64)
        Wg = jax.random.normal(k3, (E, F, D), dtype=jnp.float32) * 0.02
        Wu = jax.random.normal(k4, (E, F, D), dtype=jnp.float32) * 0.02
        Wd = jax.random.normal(k5, (E, D, F), dtype=jnp.float32) * 0.02
        return {'hidden_states': hidden_states, 'token_ids': token_ids, 'Wg': Wg, 'Wu': Wu, 'Wd': Wd}
    _L0_xattn_all = _L0_xattn_setup()
    _L0_xattn_in = {k: v for k, v in _L0_xattn_all.items() if k in ()}
    del _L0_xattn_all

    def _L0_ffn_setup():
        import jax, jax.numpy as jnp
        import numpy as np
        HIDDEN = 512
        INTER = 1408
        B, S = (2, 512)

        def _ternary(key, shape):
            return jax.random.randint(key, shape, -1, 2).astype(jnp.float32)
        key = jax.random.key(seed)
        ks = jax.random.split(key, 7)
        x = jax.random.normal(ks[0], (B, S, HIDDEN), dtype=jnp.float32)
        gate_w = _ternary(ks[1], (INTER, HIDDEN))
        up_w = _ternary(ks[2], (INTER, HIDDEN))
        down_w = _ternary(ks[3], (HIDDEN, INTER))
        gate_s = jax.random.uniform(ks[4], (INTER,), minval=0.01, maxval=0.1, dtype=jnp.float32)
        up_s = jax.random.uniform(ks[5], (INTER,), minval=0.01, maxval=0.1, dtype=jnp.float32)
        down_s = jax.random.uniform(ks[6], (HIDDEN,), minval=0.01, maxval=0.1, dtype=jnp.float32)
        return {'x': x, 'gate_w': gate_w, 'up_w': up_w, 'down_w': down_w, 'gate_s': gate_s, 'up_s': up_s, 'down_s': down_s}
    _L0_ffn_all = _L0_ffn_setup()
    _L0_ffn_in = {k: v for k, v in _L0_ffn_all.items() if k in ('gate_w', 'up_w', 'down_w', 'gate_s', 'up_s', 'down_s')}
    del _L0_ffn_all
    return {'x': x, 'itok_BxS_13_99985': itok_BxS_13_99985, 'ctx_2048': ctx_2048, 'L0_ffn_gate_w': _L0_ffn_in['gate_w'], 'L0_ffn_up_w': _L0_ffn_in['up_w'], 'L0_ffn_down_w': _L0_ffn_in['down_w'], 'L0_ffn_gate_s': _L0_ffn_in['gate_s'], 'L0_ffn_up_s': _L0_ffn_in['up_s'], 'L0_ffn_down_s': _L0_ffn_in['down_s']}

def reference(x, itok_BxS_13_99985, ctx_2048, L0_ffn_gate_w, L0_ffn_up_w, L0_ffn_down_w, L0_ffn_gate_s, L0_ffn_up_s, L0_ffn_down_s):
    import jax
    import jax.numpy as jnp

    def _L0_xattn_ref(hidden_states, token_ids, Wg, Wu, Wd):
        import jax, jax.numpy as jnp
        import numpy as np
        B, S, D = (4, 1024, 512)
        E = 4
        F = 2048 // E
        VOCAB = 25000
        tokens_per_expert = VOCAB // E
        tid = jnp.clip(token_ids, 0, VOCAB - 1)
        expert_ids = jnp.minimum(tid // tokens_per_expert, E - 1)
        out = jnp.zeros_like(hidden_states)
        for e in range(E):
            g = jax.nn.silu(jnp.einsum('bsd,fd->bsf', hidden_states, Wg[e]))
            u = jnp.einsum('bsd,fd->bsf', hidden_states, Wu[e])
            y = jnp.einsum('bsf,df->bsd', g * u, Wd[e])
            out = jnp.where((expert_ids == e)[..., None], y, out)
        return out

    def _L0_ffn_ref(x, gate_w, up_w, down_w, gate_s, up_s, down_s):
        import jax, jax.numpy as jnp
        import numpy as np
        HIDDEN = 512
        INTER = 1408
        B, S = (2, 512)

        def _ternary(key, shape):
            return jax.random.randint(key, shape, -1, 2).astype(jnp.float32)
        b, s, h = x.shape
        xf = x.reshape(b * s, h)
        g = jnp.einsum('th,ih->ti', xf, gate_w) * gate_s
        u = jnp.einsum('th,ih->ti', xf, up_w) * up_s
        hdn = jax.nn.silu(g) * u
        out = jnp.einsum('ti,hi->th', hdn, down_w) * down_s
        return out.reshape(b, s, -1)
    x = x + _L0_xattn_ref(_layernorm(x, axis=-1), itok_BxS_13_99985, ctx_2048, ctx_2048, ctx_2048)
    x = x + _L0_ffn_ref(_layernorm(x, axis=-1), L0_ffn_gate_w, L0_ffn_up_w, L0_ffn_down_w, L0_ffn_gate_s, L0_ffn_up_s, L0_ffn_down_s)
    return x

_drawn_inputs = setup_inputs


def setup_inputs(seed=0):
    import zlib

    import numpy as np

    out = dict(_drawn_inputs(seed))
    spreads = {}
    factors = {}
    for name, (base, spread) in spreads.items():
        noise = np.random.default_rng([zlib.crc32(name.encode()), seed]).standard_normal(out[name].shape)
        drawn = base * np.exp(spread * noise) if base else spread * noise
        out[name] = jnp.asarray(drawn.astype(out[name].dtype))
    for name, factor in factors.items():
        out[name] = (out[name] * factor).astype(out[name].dtype)
    return out
```

```python
from contextlib import ExitStack

import numpy as np
import concourse.bass as bass
from concourse import mybir

F32 = mybir.dt.float32
F32R = mybir.dt.float32r
F16 = mybir.dt.float16
BF16 = mybir.dt.bfloat16
I32 = mybir.dt.int32
ALU = mybir.AluOpType
ACT = mybir.ActivationFunctionType
AX = mybir.AxisListType.X

P = 128
D = 512
KD = D // P
TOKENS = 2048
TILES = TOKENS // P
EXPERTS = 4
VOCAB = 25000
PER_EXPERT = VOCAB // EXPERTS
UNITS = TILES + EXPERTS - 1
INTER = 1408
SLICES = INTER // P
SLICE_W = 3 * D
CHUNK = 512
CT = CHUNK // P
CHUNKS = TOKENS // CHUNK
EPS = 1e-5
XSCALE = 256.0

C_IDENT, C_BEFORE, C_ONES, C_SLOT = 0, P, 2 * P, 3 * P
C_TILE = 4 * P
C_TOKEN = C_TILE + TILES
C_UNIT = C_TOKEN + TILES
C_PART = C_UNIT + UNITS
C_ALL = C_PART + 1

B_G, B_U, B_ACC, B_XT = 0, 1, 2, 6
B_HT, B_UX = 2, 3


def constants():
    c = np.zeros((P, C_ALL), np.float32)
    p = np.arange(P)
    c[:, C_IDENT:C_IDENT + P] = np.eye(P)
    c[:, C_BEFORE:C_BEFORE + P] = p[:, None] < p[None, :]
    c[:, C_ONES:C_ONES + P] = 1
    c[:, C_SLOT:C_SLOT + P] = p[None, :]
    c[:, C_TILE:C_TILE + TILES] = np.arange(TILES)
    c[:, C_TOKEN:C_TOKEN + TILES] = TILES * p[:, None] + np.arange(TILES)
    c[:, C_UNIT:C_UNIT + UNITS] = np.arange(UNITS)
    c[:, C_PART] = p
    return c


def build(nc, consts, tok, x, ctx_t, ffn_w, scales, down_s, out):
    with ExitStack() as stack:
        def sb(name, shape, dt):
            return stack.enter_context(nc.sbuf_tensor(name, shape, dt))

        def sem(name):
            return stack.enter_context(nc.semaphore(name))

        cst = sb("cst", [P, C_ALL], F32)
        xs = sb("xs", [P, TILES * D], F32)
        ew = sb("ew", [P, EXPERTS * 2 * KD * D], F32R)
        w1 = sb("w1", [P, SLICES * 2 * D], BF16)
        wd = sb("wd", [P, SLICES * D], F32R)
        stage = sb("stage", [P, 2, KD * D], F32)
        xn = sb("xn", [P, 2, D], F32)
        halves = sb("halves", [P, 2, 2, D], F32R)
        gate = sb("gate", [P, D], F32)
        hid = sb("hid", [P, D], F32)
        xt = sb("xt", [P, 4, KD, CHUNK], F16)
        outb = sb("outb", [P, CT, D], F32)
        ds_row = sb("ds_row", [P, D], F32)
        gu_s = sb("gu_s", [P, 2 * SLICES], F32)
        gate_sx = sb("gate_sx", [P, 2 * SLICES], F32)
        tok_sb = sb("tok_sb", [P, TILES], I32)
        ge = sb("ge", [P, EXPERTS - 1, TILES], F32)
        member = sb("member", [P, EXPERTS, TILES], F32)
        total = sb("total", [P, EXPERTS * TILES], F32)
        zeros = sb("zeros", [P, EXPERTS * TILES], F32)
        upto = sb("upto", [P, EXPERTS * TILES], F32)
        before = sb("before", [P, EXPERTS * TILES], F32)
        rank = sb("rank", [P, EXPERTS, TILES], F32)
        pos = sb("pos", [P, TILES], F32)
        pos_i = sb("pos_i", [P, 3, TILES], I32)
        slot_f = sb("slot_f", [P, 2, TILES], F32)
        tile_hot = sb("tile_hot", [P, TILES, TILES], F32)
        tile_tok = sb("tile_tok", [P, TILES, TILES], F16)
        order = sb("order", [P, TILES], I32)
        base = sb("base", [P, EXPERTS], F32)
        edge_f = sb("edge_f", [P, 3], F32)
        edge_i = sb("edge_i", [P, 4, 3], I32)
        edge = sb("edge", [P, 5, 3], F32)
        u_ge = sb("u_ge", [P, 2, 3, UNITS], F32)
        u_red = sb("u_red", [P, 6, UNITS], F32)
        row_ge = sb("row_ge", [P, EXPERTS, UNITS], F32)
        unit_tab = sb("unit_tab", [P, 2, UNITS + 1], I32)
        mask = sb("mask", [P, UNITS], F32)
        half_neg = sb("half_neg", [P, CT], F32)
        eps = sb("eps", [P, 1], F32)
        bn6 = sb("bn6", [P, CT, 6], F32)
        mv = sb("mv", [P, CT, 2], F32)
        rstd = sb("rstd", [P, 3, CT], F32)
        mv_u = sb("mv_u", [P, 2], F32)
        bn6_u = sb("bn6_u", [P, 6], F32)
        rstd_u = sb("rstd_u", [P, 3], F32)
        inexact = sb("inexact", [P, 2 * SLICES], F32)
        inexact_p = sb("inexact_p", [P, 1], F32)
        general_i = sb("general_i", [P, 1], I32)

        ps = stack.enter_context(nc.psum_tensor("ps", [P, 8, 512], F32))

        cst_in = sem("cst_in")
        tok_in = sem("tok_in")
        scale_in = sem("scale_in")
        expert_in = [sem(f"expert_in{e}") for e in range(EXPERTS)]
        slice_in = sem("slice_in")
        slice_used = sem("slice_used")
        slice_short = sem("slice_short")
        x_in = [sem("x_in0"), sem("x_in1"), sem("x_in_rest")]
        out_done = [sem(f"out_done{t}") for t in range(CT)]
        out_free = sem("out_free")
        again_in = sem("again_in")
        again_used = sem("again_used")
        dve_step = sem("dve_step")
        pool_step = sem("pool_step")
        rest_used = sem("rest_used")
        member_ready = sem("member_ready")
        counts_ready = sem("counts_ready")
        hot_ready = sem("hot_ready")
        order_psum = sem("order_psum")
        order_ready = sem("order_ready")
        units_ready = sem("units_ready")
        half_ready = sem("half_ready")
        expert_high = sem("expert_high")
        expert_low = sem("expert_low")
        count_ready = sem("count_ready")
        count_psum = sem("count_psum")
        general_ready = sem("general_ready")
        u_bn = sem("u_bn")
        u_stats = sem("u_stats")
        u_rstd = sem("u_rstd")
        u_norm = sem("u_norm")
        u_xt = sem("u_xt")
        u_xt_high = sem("u_xt_high")
        u_xt_low = sem("u_xt_low")
        u_up = sem("u_up")
        u_silu = sem("u_silu")
        u_hid = sem("u_hid")
        u_ht = sem("u_ht")
        u_ht_high = sem("u_ht_high")
        u_ht_low = sem("u_ht_low")
        u_down = sem("u_down")
        x_now = sem("x_now")
        c_bn = sem("c_bn")
        c_stats = sem("c_stats")
        c_rstd = sem("c_rstd")
        t_norm = sem("t_norm")
        t_xt = sem("t_xt")
        t_high = sem("t_high")
        t_low = sem("t_low")
        s_gate = sem("s_gate")
        s_up = sem("s_up")
        s_silu = sem("s_silu")
        s_hid = sem("s_hid")
        s_high = sem("s_high")
        s_low = sem("s_low")
        s_rest = sem("s_rest")
        s_down = sem("s_down")
        acc_full = sem("acc_full")
        acc_free = sem("acc_free")
        out_ready = sem("out_ready")

        ident = cst[:, C_IDENT:C_IDENT + P]
        slot_hot = xt[:, 0, :, :].rearrange("p k t -> p (k t)").rearrange("p (c s) -> p c s", s=P)
        dump = xt[:, 2, 0:2, :].rearrange("p k t -> p (k t)")
        rest_gu = [stage[:, 1, j * D:(j + 1) * D].bitcast(BF16) for j in range(2)]

        def rest_d(i):
            return ew[:, (i % 2) * D:(i % 2 + 1) * D]

        def ew_at(e, part, k):
            return ew[:, bass.ds(e * (2 * KD * D) + (part * KD + k) * D, D)]

        def xs_at(q):
            return xs[:, bass.ds(q * D, D)]

        def cols(a, n=P):
            return slice(a * n, (a + 1) * n)

        block = stack.enter_context(nc.Block())

        @block.sync
        def _(sp):
            sp.dma_start(tok_sb[:, :], tok).then_inc(tok_in, 16)
            sp.dma_start(cst[:, :], consts).then_inc(cst_in, 16)
            for e in range(EXPERTS):
                if e >= 2:
                    sp.wait_ge(expert_low, e - 1)
                sp.dma_start(stage[:, e % 2, :], ctx_t[e]).then_inc(expert_in[e], 16)
            sp.dma_start(gu_s[:, :], scales).then_inc(scale_in, 16)
            sp.dma_start(ds_row[:, :], down_s).then_inc(scale_in, 16)
            sp.wait_ge(expert_low, EXPERTS)
            for s in range(SLICES):
                if s >= 1:
                    sp.wait_ge(slice_in, 16 * s)
                if s >= 2:
                    sp.wait_ge(slice_used, s - 1)
                sp.dma_start(stage[:, s % 2, 0:SLICE_W], ffn_w[s]).then_inc(slice_in, 16)
            sp.wait_ge(general_ready, 1)
            general = sp.value_load(general_i[0:1, 0:1])
            with sp.If(general):
                with sp.Fori(0, CHUNKS) as c:
                    for s in range(SLICES):
                        sp.wait_ge(again_used, c * SLICES + s + 1)
                        sp.dma_start(stage[:, 0, 0:SLICE_W], ffn_w[s]).then_inc(again_in, 16)
            with sp.Else():
                pass

        def chunk_rstd(pool, c):
            pool.wait_ge(c_stats, c + 1)
            pool.tensor_scalar(rstd[:, 0, :], mv[:, :, 1:2].rearrange("p t a -> p (t a)"), EPS, None,
                               ALU.add).then_inc(pool_step, 1)
            pool.wait_ge(pool_step, 2 * UNITS + 2 * c + 1)
            pool.tensor_tensor(rstd[:, 1, :], rstd[:, 0, :], half_neg[:, :], ALU.pow).then_inc(pool_step, 1)
            pool.wait_ge(pool_step, 2 * UNITS + 2 * c + 2)
            pool.tensor_scalar(rstd[:, 2, :], rstd[:, 1, :], XSCALE, None, ALU.mult).then_inc(c_rstd, 1)

        @block.gpsimd
        def _(pool):
            pool.sem_inc(again_used, 1)
            pool.sem_inc(s_down, 1)
            pool.sem_inc(out_free, CT)
            pool.memset(half_neg[:, :], -0.5).then_inc(half_ready, 1)
            pool.memset(eps[:, :], EPS).then_inc(half_ready, 1)
            pool.wait_ge(order_ready, 1)
            for q in range(TILES):
                pool.indirect_dma_start(
                    xs[:, q * D:(q + 1) * D], None, x,
                    bass.IndirectOffsetOnAxis(ap=order[:, q:q + 1], axis=0)).then_inc(x_in[min(q, 2)], 16)
            pool.wait_ge(half_ready, 2)
            pool.wait_ge(units_ready, 1)
            with pool.Fori(0, UNITS) as u:
                pool.wait_ge(u_stats, u + 1)
                pool.tensor_tensor(rstd_u[:, 0:1], mv_u[:, 1:2], eps[:, :], ALU.add).then_inc(pool_step, 1)
                pool.wait_ge(pool_step, 2 * u + 1)
                pool.tensor_tensor(rstd_u[:, 1:2], rstd_u[:, 0:1], half_neg[:, 0:1], ALU.pow).then_inc(pool_step, 1)
                pool.wait_ge(pool_step, 2 * u + 2)
                pool.tensor_tensor(rstd_u[:, 2:3], rstd_u[:, 1:2], mask[:, bass.ds(u, 1)],
                                   ALU.mult).then_inc(u_rstd, 1)
            for c in range(CHUNKS):
                if c == 0:
                    chunk_rstd(pool, 0)
                if c + 1 < CHUNKS:
                    chunk_rstd(pool, c + 1)
                for t in range(CT):
                    q = c * CT + t
                    pool.wait_ge(out_ready, q + 1)
                    pool.indirect_dma_start(
                        out, bass.IndirectOffsetOnAxis(ap=order[:, q:q + 1], axis=0),
                        outb[:, t, :], None).then_inc(out_done[t], 16)
                for t in range(CT):
                    pool.wait_ge(out_done[t], 16 * c + 16)
                    pool.sem_inc(out_free, 1)

        @block.scalar
        def _(act):
            for e in range(EXPERTS):
                act.wait_ge(expert_in[e], 16)
                act.activation(ew[:, e * 2 * KD * D:(e * 2 + 1) * KD * D], stage[:, e % 2, :],
                               ACT.Copy).then_inc(expert_high, 1)

            def xt_high(u):
                act.wait_ge(u_xt, u + 1)
                act.activation(halves[:, 0, 0, :], ps[:, B_UX, :], ACT.Copy).then_inc(u_xt_high, 1)

            def silu(u):
                act.wait_ge(u_up, u + 1)
                act.activation(gate[:, :], ps[:, B_G, :], ACT.Silu).then_inc(u_silu, 1)

            def ht_high(u):
                act.wait_ge(u_ht, u + 1)
                act.activation(halves[:, 1, 0, :], ps[:, B_HT, :], ACT.Copy).then_inc(u_ht_high, 1)

            def shorten(s):
                act.wait_ge(slice_in, 16 * s + 16)
                act.activation(w1[:, bass.ds(s * (2 * D), 2 * D)],
                               stage[:, bass.ds(s % 2, 1), 0:2 * D].rearrange("p a w -> p (a w)"),
                               ACT.Copy).then_inc(slice_short, 1)
                act.activation(wd[:, bass.ds(s * D, D)],
                               stage[:, bass.ds(s % 2, 1), 2 * D:3 * D].rearrange("p a w -> p (a w)"),
                               ACT.Copy).then_inc(slice_short, 1)

            xt_high(0)
            silu(0)
            xt_high(1)
            with act.Fori(1, SLICES + 1) as u:
                ht_high(u - 1)
                silu(u)
                xt_high(u + 1)
                shorten(u - 1)
            with act.Fori(SLICES + 1, UNITS - 1) as u:
                ht_high(u - 1)
                silu(u)
                xt_high(u + 1)

            def tile_high(t, slot, tt):
                act.wait_ge(t_xt, t + 1)
                act.activation(xt[:, bass.ds(2 * slot, 1), :, cols(tt)].rearrange("p a k t -> p (a k) t"),
                               ps[:, B_XT + tt % 2, :].rearrange("p (k t) -> p k t", k=KD),
                               ACT.Copy).then_inc(t_high, 1)

            ht_high(UNITS - 2)
            silu(UNITS - 1)
            tile_high(0, 0, 0)
            ht_high(UNITS - 1)
            for t in range(1, CT):
                tile_high(t, 0, t)

            def chunk(c, last):
                for i in range(SLICES):
                    n = c * SLICES + i
                    act.wait_ge(s_gate, n + 1)
                    if i >= 1:
                        act.wait_ge(s_hid, n)
                    act.activation(gate[:, :], ps[:, B_G, :], ACT.Silu, scale=gate_sx[:, i:i + 1]).then_inc(s_silu, 1)
                    act.wait_ge(s_hid, n + 1)
                    act.activation(halves[:, i % 2, 0, :], hid[:, :], ACT.Copy).then_inc(s_high, 1)
                    if not last and i % 2 == 1 and i < 2 * CT:
                        tile_high(c * CT + CT + i // 2, (c + 1) % 2, i // 2)

            with act.Fori(0, CHUNKS - 1) as c:
                chunk(c, False)
            chunk(CHUNKS - 1, True)

        @block.vector
        def _(dve):
            steps = [0]

            def step(ins):
                steps[0] += 1
                ins.then_inc(dve_step, 1)
                dve.wait_ge(dve_step, steps[0])

            step(dve.memset(zeros[:, :], 0.0))
            step(dve.memset(base[:, 3:4], float(TOKENS)))
            dve.wait_ge(tok_in, 16)
            for e in range(1, EXPERTS):
                step(dve.tensor_scalar(ge[:, e - 1, :], tok_sb[:, :], float(e * PER_EXPERT), None, ALU.is_ge))
            step(dve.tensor_scalar(member[:, 0, :], ge[:, 0, :], -1.0, 1.0, ALU.mult, ALU.add))
            step(dve.tensor_tensor(member[:, 1:3, :], ge[:, 0:2, :], ge[:, 1:3, :], ALU.subtract))
            dve.tensor_copy(member[:, 3, :], ge[:, 2, :]).then_inc(member_ready, 1)
            dve.wait_ge(counts_ready, 1)
            step(dve.tensor_copy(total[:, :], ps[:, B_ACC + 2, 0:EXPERTS * TILES]))
            step(dve.tensor_tensor_scan(upto[:, :], total[:, :], zeros[:, :], 0.0, ALU.add, ALU.add))
            step(dve.tensor_tensor(before[:, :], upto[:, :], total[:, :], ALU.subtract))
            step(dve.tensor_tensor(rank[:, :, :].rearrange("p e c -> p (e c)"),
                                   ps[:, B_ACC + 2, P:P + EXPERTS * TILES], before[:, :], ALU.add))
            step(dve.tensor_tensor(rank[:, :, :], rank[:, :, :], member[:, :, :], ALU.mult))
            step(dve.tensor_reduce(pos[:, :], rank[:, :, :].rearrange("p e c -> p c e"), AX, ALU.add))
            step(dve.tensor_copy(pos_i[:, 0, :], pos[:, :]))
            step(dve.tensor_scalar(pos_i[:, 1, :], pos_i[:, 0, :], P - 1, None, ALU.bitwise_and))
            step(dve.tensor_scalar(pos_i[:, 2, :], pos_i[:, 0, :], 7, None, ALU.logical_shift_right))
            step(dve.tensor_copy(slot_f[:, :, :], pos_i[:, 1:3, :]))
            dve.wait_ge(cst_in, 16)
            step(dve.tensor_tensor(slot_hot, slot_f[:, 0, :].unsqueeze(2).broadcast_to([P, TILES, P]),
                                   cst[:, C_SLOT:C_SLOT + P].unsqueeze(1).broadcast_to([P, TILES, P]),
                                   ALU.is_equal))
            step(dve.tensor_tensor(tile_hot[:, :, :], slot_f[:, 1, :].unsqueeze(2).broadcast_to([P, TILES, TILES]),
                                   cst[:, C_TILE:C_TILE + TILES].unsqueeze(1).broadcast_to([P, TILES, TILES]),
                                   ALU.is_equal))
            dve.tensor_tensor(tile_tok[:, :, :], tile_hot[:, :, :],
                              cst[:, C_TOKEN:C_TOKEN + TILES].unsqueeze(2).broadcast_to([P, TILES, TILES]),
                              ALU.mult).then_inc(hot_ready, 1)
            step(dve.tensor_copy(base[:, 0:3], before[:, TILES::TILES]))
            step(dve.tensor_scalar(edge_f[:, :], base[:, 0:3], float(P - 1), None, ALU.add))
            step(dve.tensor_copy(edge_i[:, 0, :], base[:, 0:3]))
            step(dve.tensor_copy(edge_i[:, 1, :], edge_f[:, :]))
            step(dve.tensor_scalar(edge_i[:, 2:4, :], edge_i[:, 0:2, :], 7, None, ALU.logical_shift_right))
            step(dve.tensor_copy(edge[:, 0:2, :], edge_i[:, 2:4, :]))
            step(dve.tensor_tensor(edge[:, 2, :], edge[:, 0, :], edge[:, 1, :], ALU.subtract))
            step(dve.tensor_tensor_scan(edge[:, 3, :], edge[:, 2, :], zeros[:, 0:3], 0.0, ALU.add, ALU.add))
            step(dve.tensor_tensor(edge[:, 3, :], edge[:, 3, :], edge[:, 2, :], ALU.subtract))
            step(dve.tensor_tensor(edge[:, 4, :], edge[:, 1, :], edge[:, 3, :], ALU.subtract))

            dve.wait_ge(order_psum, 1)
            dve.tensor_copy(order[:, :], ps[:, B_ACC + 3, 0:TILES]).then_inc(order_ready, 1)

            unit_row = cst[:, C_UNIT:C_UNIT + UNITS]
            step(dve.tensor_tensor(u_ge[:, 0, :, :], unit_row.unsqueeze(1).broadcast_to([P, 3, UNITS]),
                                   edge[:, 4, :].unsqueeze(2).broadcast_to([P, 3, UNITS]), ALU.is_ge))
            step(dve.tensor_tensor(u_ge[:, 1, :, :], u_ge[:, 0, :, :],
                                   edge[:, 2, :].unsqueeze(2).broadcast_to([P, 3, UNITS]), ALU.mult))
            step(dve.tensor_reduce(u_red[:, 0, :], u_ge[:, 0, :, :].rearrange("p e u -> p u e"), AX, ALU.add))
            step(dve.tensor_reduce(u_red[:, 1, :], u_ge[:, 1, :, :].rearrange("p e u -> p u e"), AX, ALU.add))
            step(dve.tensor_tensor(u_red[:, 2, :], u_red[:, 1, :], unit_row, ALU.add))
            step(dve.tensor_scalar(u_red[:, 3, :], u_red[:, 2, :], float(P), cst[:, C_PART:C_PART + 1],
                                   ALU.mult, ALU.add))
            step(dve.tensor_tensor(row_ge[:, :, :], u_red[:, 3, :].unsqueeze(1).broadcast_to([P, EXPERTS, UNITS]),
                                   base[:, :].unsqueeze(2).broadcast_to([P, EXPERTS, UNITS]), ALU.is_ge))
            step(dve.tensor_reduce(u_red[:, 4, :], row_ge[:, :, :].rearrange("p e u -> p u e"), AX, ALU.add))
            step(dve.tensor_tensor(mask[:, :], u_red[:, 4, :], u_red[:, 0, :], ALU.is_equal))
            step(dve.tensor_scalar(u_red[:, 5, :], u_red[:, 2, :], float(TILES - 1), None, ALU.min))
            step(dve.tensor_copy(unit_tab[:, 0, 0:UNITS], u_red[:, 5, :]))
            dve.tensor_copy(unit_tab[:, 1, 0:UNITS], u_red[:, 0, :]).then_inc(units_ready, 1)
            dve.wait_ge(units_ready, 1)

            for e in range(EXPERTS):
                dve.wait_ge(expert_high, e + 1)
                dve.tensor_tensor(ew[:, (e * 2 + 1) * KD * D:(e * 2 + 2) * KD * D], stage[:, e % 2, :],
                                  ew[:, e * 2 * KD * D:(e * 2 + 1) * KD * D].bitcast(F32),
                                  ALU.subtract).then_inc(expert_low, 1)
            dve.wait_ge(scale_in, 32)
            dve.tensor_scalar(gate_sx[:, :], gu_s[:, :], 1.0 / XSCALE, None, ALU.mult).then_inc(x_now, 1)

            def tile_of(u):
                return dve.value_load(unit_tab[0:1, 0, bass.ds(u, 1)], min_val=0, max_val=TILES - 1)

            def stats(u, q):
                dve.bn_stats(bn6_u[:, :], xs_at(q)).then_inc(u_bn, 1)

            def aggregate():
                dve.bn_aggr(mv_u[:, :], bn6_u[:, :]).then_inc(u_stats, 1)

            def norm(u, q):
                dve.wait_ge(u_rstd, u + 1)
                dve.tensor_scalar(xn[:, 0, :], xs_at(q), mv_u[:, 0:1], rstd_u[:, 2:3],
                                  ALU.subtract, ALU.mult).then_inc(u_norm, 1)

            def xt_low(u):
                dve.wait_ge(u_xt_high, u + 1)
                dve.tensor_tensor(halves[:, 0, 1, :], ps[:, B_UX, :], halves[:, 0, 0, :].bitcast(F32),
                                  ALU.subtract).then_inc(u_xt_low, 1)

            def hidden(u):
                dve.wait_ge(u_silu, u + 1)
                dve.tensor_tensor(hid[:, :], ps[:, B_G, :], gate[:, :], ALU.mult).then_inc(u_hid, 1)

            def ht_low(u):
                dve.wait_ge(u_ht_high, u + 1)
                dve.tensor_tensor(halves[:, 1, 1, :], ps[:, B_HT, :], halves[:, 1, 0, :].bitcast(F32),
                                  ALU.subtract).then_inc(u_ht_low, 1)

            def add(u, q):
                dve.wait_ge(u_down, u + 1)
                dve.tensor_tensor(xs_at(q), ps[:, B_U, :], xs_at(q), ALU.add).then_inc(x_now, 1)

            def compare(s):
                dve.wait_ge(slice_short, 2 * s + 2)
                raw = stage[:, bass.ds(s % 2, 1), 0:SLICE_W].rearrange("p a w -> p (a w)")
                dve.scalar_tensor_tensor(dump, raw[:, 0:2 * D], 1.0, w1[:, bass.ds(s * (2 * D), 2 * D)],
                                         ALU.mult, ALU.not_equal,
                                         accum_out=inexact[:, bass.ds(2 * s, 1)]).then_inc(count_ready, 1)
                dve.wait_ge(count_ready, 2 * s + 1)
                dve.scalar_tensor_tensor(dump[:, 0:D], raw[:, 2 * D:3 * D], 1.0,
                                         wd[:, bass.ds(s * D, D)].bitcast(F32), ALU.mult, ALU.not_equal,
                                         accum_out=inexact[:, bass.ds(2 * s + 1, 1)]).then_inc(count_ready, 1)
                dve.wait_ge(count_ready, 2 * s + 2)
                dve.sem_inc(slice_used, 1)

            def unit(u):
                ht_low(u - 1)
                dve.wait_ge(x_now, u)
                norm(u + 1, tile_of(u + 1))
                hidden(u)
                xt_low(u + 1)

            dve.wait_ge(x_in[0], 16)
            stats(0, tile_of(0))
            dve.wait_ge(u_bn, 1)
            aggregate()
            norm(0, tile_of(0))
            xt_low(0)
            dve.wait_ge(x_in[1], 16)
            stats(1, tile_of(1))
            dve.wait_ge(u_bn, 2)
            aggregate()
            norm(1, tile_of(1))
            hidden(0)
            xt_low(1)
            dve.wait_ge(x_in[2], 16 * (TILES - 2))
            stats(2, tile_of(2))
            dve.wait_ge(u_bn, 3)
            aggregate()
            with dve.Fori(1, SLICES + 1) as u:
                unit(u)
                dve.wait_ge(x_now, u)
                stats(u + 2, tile_of(u + 2))
                dve.wait_ge(u_bn, u + 3)
                add(u - 1, tile_of(u - 1))
                aggregate()
                compare(u - 1)
            with dve.Fori(SLICES + 1, UNITS - 2) as u:
                unit(u)
                dve.wait_ge(x_now, u)
                stats(u + 2, tile_of(u + 2))
                dve.wait_ge(u_bn, u + 3)
                add(u - 1, tile_of(u - 1))
                aggregate()
            unit(UNITS - 2)
            dve.tensor_reduce(inexact_p[:, :], inexact[:, :], AX, ALU.add).then_inc(count_ready, 1)
            add(UNITS - 3, tile_of(UNITS - 3))

            def chunk_stats(c, t):
                dve.bn_stats(bn6[:, t, :], xs_at(c * CT + t)).then_inc(c_bn, 1)

            def chunk_aggr(t):
                ins = dve.bn_aggr(mv[:, t, :], bn6[:, t, :])
                if t == CT - 1:
                    ins.then_inc(c_stats, 1)

            def tile_norm(c, t):
                n = c * CT + t
                dve.wait_ge(c_rstd, c + 1)
                dve.tensor_scalar(xn[:, t % 2, :], xs_at(n), mv[:, t, 0:1], rstd[:, 2, t:t + 1],
                                  ALU.subtract, ALU.mult).then_inc(t_norm, 1)

            def tile_low(c, slot, t):
                n = c * CT + t
                dve.wait_ge(t_high, n + 1)
                dve.tensor_tensor(xt[:, bass.ds(2 * slot + 1, 1), :, cols(t)].rearrange("p a k t -> p (a k) t"),
                                  ps[:, B_XT + t % 2, :].rearrange("p (k t) -> p k t", k=KD),
                                  xt[:, bass.ds(2 * slot, 1), :, cols(t)].rearrange("p a k t -> p (a k) t"),
                                  ALU.subtract).then_inc(t_low, 1)

            ht_low(UNITS - 2)
            dve.wait_ge(x_now, UNITS - 1)
            for t in range(CT):
                chunk_stats(0, t)
            dve.wait_ge(c_bn, CT)
            for t in range(CT):
                chunk_aggr(t)
            dve.wait_ge(u_xt, UNITS)
            tile_norm(0, 0)
            hidden(UNITS - 1)
            tile_low(0, 0, 0)
            tile_norm(0, 1)
            add(UNITS - 2, tile_of(UNITS - 2))
            ht_low(UNITS - 1)
            tile_low(0, 0, 1)
            dve.wait_ge(t_xt, 1)
            tile_norm(0, 2)
            dve.wait_ge(count_psum, 1)
            dve.tensor_copy(general_i[0:1, 0:1], ps[0:1, B_ACC + 3, 0:1]).then_inc(general_ready, 1)
            dve.wait_ge(x_now, UNITS)
            add(UNITS - 1, tile_of(UNITS - 1))
            dve.wait_ge(x_now, UNITS + 1)
            dve.sem_inc(acc_free, 1)
            tile_low(0, 0, 2)
            dve.wait_ge(t_xt, 2)
            tile_norm(0, 3)
            tile_low(0, 0, 3)
            dve.wait_ge(general_ready, 1)
            general = dve.value_load(general_i[0:1, 0:1])

            def remainders(c, i):
                n = c * SLICES + i
                raw_gu, raw_d = stage[:, 0, 0:2 * D], stage[:, 0, 2 * D:3 * D]
                dve.wait_ge(again_in, 16 * n + 16)
                dve.wait_ge(s_down, c * SLICES + max(i, 1))
                if i >= 1:
                    dve.wait_ge(s_up, n)
                dve.tensor_tensor(raw_gu, raw_gu, w1[:, i * 2 * D:(i + 1) * 2 * D],
                                  ALU.subtract).then_inc(rest_used, 1)
                dve.wait_ge(rest_used, 2 * n + 1)
                dve.tensor_copy(rest_gu[0], raw_gu).then_inc(rest_used, 1)
                dve.wait_ge(rest_used, 2 * n + 2)
                dve.tensor_tensor(rest_gu[1], raw_gu, rest_gu[0], ALU.subtract)
                dve.tensor_tensor(rest_d(i), raw_d, wd[:, i * D:(i + 1) * D].bitcast(F32),
                                  ALU.subtract).then_inc(s_rest, 1)
                dve.wait_ge(s_rest, n + 1)
                dve.sem_inc(again_used, 1)

            def chunk(c, last, rest):
                for i in range(SLICES):
                    n = c * SLICES + i
                    if rest:
                        remainders(c, i)
                    if not last and i == 1:
                        dve.wait_ge(c_bn, CT * c + 2 * CT)
                    if i >= 1:
                        dve.wait_ge(s_low, n)
                    dve.wait_ge(s_up, n + 1)
                    dve.wait_ge(s_silu, n + 1)
                    dve.scalar_tensor_tensor(hid[:, :], ps[:, B_U, :], gate_sx[:, SLICES + i:SLICES + i + 1],
                                             gate[:, :], ALU.mult, ALU.mult).then_inc(s_hid, 1)
                    if not last:
                        if i == 0:
                            for t in range(CT):
                                chunk_stats(c + 1, t)
                        if i == 1:
                            for t in range(CT):
                                chunk_aggr(t)
                        if i % 2 == 1 and i < 2 * CT:
                            dve.wait_ge(t_xt, c * CT + CT + i // 2 - 1)
                            tile_norm(c + 1, i // 2)
                    dve.wait_ge(s_high, n + 1)
                    dve.tensor_tensor(halves[:, i % 2, 1, :], hid[:, :], halves[:, i % 2, 0, :].bitcast(F32),
                                      ALU.subtract).then_inc(s_low, 1)
                    if not last and i % 2 == 1 and i < 2 * CT:
                        tile_low(c + 1, (c + 1) % 2, i // 2)
                for t in range(CT):
                    dve.wait_ge(acc_full, c * CT + t + 1)
                    dve.wait_ge(out_free, c * CT + t + 1)
                    dve.tensor_tensor(outb[:, t, :], ps[:, B_ACC + t, :], ds_row[:, :],
                                      ALU.mult).then_inc(acc_free, 1)
                for t in range(CT):
                    dve.wait_ge(acc_free, c * CT + t + 2)
                    dve.tensor_tensor(outb[:, t, :], outb[:, t, :], xs_at(c * CT + t),
                                      ALU.add).then_inc(out_ready, 1)

            def dense(rest):
                with dve.Fori(0, CHUNKS - 1) as c:
                    chunk(c, False, rest)
                chunk(CHUNKS - 1, True, rest)

            with dve.If(general):
                dense(True)
            with dve.Else():
                dense(False)

        @block.tensor
        def _(pe):
            pe.wait_ge(cst_in, 16)
            pe.wait_ge(member_ready, 1)
            members = member[:, :, :].rearrange("p e c -> p (e c)")
            n_cols = EXPERTS * TILES
            pe.matmul(ps[:, B_ACC + 2, 0:n_cols], cst[:, C_ONES:C_ONES + P], members, start=True, stop=True)
            pe.matmul(ps[:, B_ACC + 2, P:P + n_cols], cst[:, C_BEFORE:C_BEFORE + P], members,
                      start=True, stop=True).then_inc(counts_ready, 1)
            pe.wait_ge(hot_ready, 1)
            for c in range(TILES):
                mm = pe.matmul(ps[:, B_ACC + 3, 0:TILES], slot_hot[:, c, :], tile_tok[:, c, :],
                               start=(c == 0), stop=(c == TILES - 1))
            mm.then_inc(order_psum, 1)
            pe.wait_ge(units_ready, 1)
            pe.wait_ge(expert_low, EXPERTS)

            def expert_of(u):
                return pe.value_load(unit_tab[0:1, 1, bass.ds(u, 1)], min_val=0, max_val=EXPERTS - 1)

            def split_product(dst, slot, e):
                passes = [(k, a, b) for k in range(KD) for a, b in ((0, 0), (0, 1), (1, 0))]
                for n, (k, a, b) in enumerate(passes):
                    mm = pe.matmul(dst, halves[:, slot, a, cols(k)], ew_at(e, b, k),
                                   start=(n == 0), stop=(n == len(passes) - 1))
                return mm

            def turn(bank, src):
                for k in range(KD):
                    mm = pe.transpose(ps[:, bank, cols(k)], src[:, cols(k)], ident)
                return mm

            def turn_x(u):
                pe.wait_ge(u_norm, u + 1)
                turn(B_UX, xn[:, 0, :]).then_inc(u_xt, 1)

            def up(u):
                pe.wait_ge(u_xt_low, u + 1)
                split_product(ps[:, B_G, :], 0, expert_of(u)).then_inc(u_up, 1)

            def turn_h(u):
                pe.wait_ge(u_hid, u + 1)
                turn(B_HT, hid).then_inc(u_ht, 1)

            def down(u):
                pe.wait_ge(u_ht_low, u + 1)
                pe.wait_ge(x_now, u + 1)
                split_product(ps[:, B_U, :], 1, expert_of(u)).then_inc(u_down, 1)

            turn_x(0)
            up(0)
            turn_x(1)
            turn_h(0)
            with pe.Fori(1, UNITS - 1) as u:
                up(u)
                turn_x(u + 1)
                down(u - 1)
                turn_h(u)

            def turn_tile(t, tt):
                pe.wait_ge(t_norm, t + 1)
                turn(B_XT + tt % 2, xn[:, tt % 2, :]).then_inc(t_xt, 1)

            up(UNITS - 1)
            turn_tile(0, 0)
            down(UNITS - 2)
            turn_h(UNITS - 1)
            turn_tile(1, 1)
            pe.wait_ge(count_ready, 2 * SLICES + 1)
            pe.matmul(ps[:, B_ACC + 3, 0:1], cst[:, C_ONES:C_ONES + P], inexact_p[:, :],
                      start=True, stop=True).then_inc(count_psum, 1)
            down(UNITS - 1)
            for t in range(2, CT):
                pe.wait_ge(t_low, t - 1)
                turn_tile(t, t)
            pe.wait_ge(general_ready, 1)
            general = pe.value_load(general_i[0:1, 0:1])

            def gate_or_up(bank, i, which, slot, rest):
                at = (i * 2 + which) * D
                parts = []
                for k in range(KD):
                    parts += [(w1[:, at + k * P:at + (k + 1) * P], 0, k), (w1[:, at + k * P:at + (k + 1) * P], 1, k)]
                    if rest:
                        r = [rest_gu[j][:, which * D + k * P:which * D + (k + 1) * P] for j in range(2)]
                        parts += [(r[0], 0, k), (r[0], 1, k), (r[1], 0, k)]
                for n, (w, part, k) in enumerate(parts):
                    mm = pe.matmul(ps[:, bank, :], w,
                                   xt[:, bass.ds(2 * slot + part, 1), k, :].rearrange("p a t -> p (a t)"),
                                   start=(n == 0), stop=(n == len(parts) - 1))
                return mm

            def slice_down(c, i, rest):
                n = c * SLICES + i
                pe.wait_ge(s_low, n + 1)
                if i == 0:
                    pe.wait_ge(acc_free, c * CT + 1)
                for t in range(CT):
                    rhs = wd[:, i * D:(i + 1) * D]
                    pairs = [(0, rhs), (1, rhs)]
                    if rest:
                        pairs += [(0, rest_d(i)), (1, rest_d(i))]
                    for m, (part, r) in enumerate(pairs):
                        mm = pe.matmul(ps[:, B_ACC + t, :], halves[:, i % 2, part, cols(t)], r,
                                       start=(i == 0 and m == 0), stop=(i == SLICES - 1 and m == len(pairs) - 1))
                    if i == SLICES - 1:
                        mm.then_inc(acc_full, 1)
                if rest:
                    pe.matmul(ps[:, B_XT, 0:64], cst[:, C_ONES:C_ONES + P], cst[:, 0:64],
                              start=True, stop=True).then_inc(s_down, 1)

            def chunk(c, last, rest):
                slot = c % 2
                for i in range(SLICES):
                    n = c * SLICES + i
                    if i == 0:
                        pe.wait_ge(t_low, c * CT + CT)
                    else:
                        pe.wait_ge(s_silu, n)
                    if rest:
                        pe.wait_ge(s_rest, n + 1)
                    gate_or_up(B_G, i, 0, slot, rest).then_inc(s_gate, 1)
                    if i >= 1:
                        pe.wait_ge(s_hid, n)
                    elif not isinstance(c, int) or c == 0:
                        pe.wait_ge(x_now, UNITS + 1)
                    gate_or_up(B_U, i, 1, slot, rest).then_inc(s_up, 1)
                    if not last and i % 2 == 1 and i < 2 * CT:
                        pe.wait_ge(t_low, c * CT + CT + i // 2 - 1)
                        turn_tile(c * CT + CT + i // 2, i // 2)
                    if i >= 1:
                        slice_down(c, i - 1, rest)
                slice_down(c, SLICES - 1, rest)

            def dense(rest):
                with pe.Fori(0, CHUNKS - 1) as c:
                    chunk(c, False, rest)
                chunk(CHUNKS - 1, True, rest)

            with pe.If(general):
                dense(True)
            with pe.Else():
                dense(False)


def kernel(x, itok_BxS_13_99985, ctx_2048, L0_ffn_gate_w, L0_ffn_up_w, L0_ffn_down_w,
           L0_ffn_gate_s, L0_ffn_up_s, L0_ffn_down_s):
    import concourse.bacc as bacc
    from concourse.bass_utils import run_bass_kernel_spmd

    x = np.asarray(x)
    shape = x.shape

    def by_slice(w):
        return np.asarray(w).reshape(SLICES, P, KD, P).transpose(0, 3, 2, 1).reshape(SLICES, P, D)

    down = np.asarray(L0_ffn_down_w).T.reshape(SLICES, P, D)
    arrays = {
        "consts": constants(),
        "tok": np.asarray(itok_BxS_13_99985).reshape(P, TILES),
        "x_rows": x.reshape(TOKENS, D),
        "ctx_t": np.asarray(ctx_2048).transpose(0, 2, 1).reshape(EXPERTS, KD, P, D)
                   .transpose(0, 2, 1, 3).reshape(EXPERTS, P, KD * D),
        "ffn_w": np.concatenate([by_slice(L0_ffn_gate_w), by_slice(L0_ffn_up_w), down], axis=2),
        "scales": np.concatenate([np.asarray(L0_ffn_gate_s).reshape(SLICES, P).T,
                                  np.asarray(L0_ffn_up_s).reshape(SLICES, P).T], axis=1),
        "down_s": np.broadcast_to(np.asarray(L0_ffn_down_s)[None, :], (P, D)),
    }
    arrays = {k: np.ascontiguousarray(a) for k, a in arrays.items()}
    nc = bacc.Bacc("TRN2", target_bir_lowering=False, num_devices=1)
    args = [nc.dram_tensor(k, a.shape, mybir.dt.from_np(a.dtype), kind="ExternalInput").ap()
            for k, a in arrays.items()]
    res = nc.dram_tensor("y_rows", (TOKENS, D), F32, kind="ExternalOutput").ap()
    build(nc, *args, res)
    r = run_bass_kernel_spmd(nc, [arrays], core_ids=[0])
    return r.results[0]["y_rows"].reshape(shape)
```

```python
from contextlib import ExitStack

import numpy as np
import concourse.bass as bass
from concourse import mybir

F32 = mybir.dt.float32
F32R = mybir.dt.float32r
F16 = mybir.dt.float16
BF16 = mybir.dt.bfloat16
I32 = mybir.dt.int32
ALU = mybir.AluOpType
ACT = mybir.ActivationFunctionType
AX = mybir.AxisListType.X

P = 128
D = 512
KD = D // P
TOKENS = 2048
TILES = TOKENS // P
EXPERTS = 4
VOCAB = 25000
PER_EXPERT = VOCAB // EXPERTS
UNITS = TILES + EXPERTS - 1
INTER = 1408
SLICES = INTER // P
SLICE_W = 3 * D
CHUNK = 512
CT = CHUNK // P
CHUNKS = TOKENS // CHUNK
TURN_AT = [3, 5, 7, 10]
NORM_AT = [2, 4, 6, 8]
FIRST = 3
EPS = 1e-5
XSCALE = 256.0

C_IDENT, C_BEFORE, C_ONES, C_SLOT = 0, P, 2 * P, 3 * P
C_TILE = 4 * P
C_TOKEN = C_TILE + TILES
C_UNIT = C_TOKEN + TILES
C_PART = C_UNIT + UNITS
C_ALL = C_PART + 1

B_G, B_U, B_ACC, B_XT = 0, 1, 2, 6
B_HT, B_UX = 2, 3


def constants():
    c = np.zeros((P, C_ALL), np.float32)
    p = np.arange(P)
    c[:, C_IDENT:C_IDENT + P] = np.eye(P)
    c[:, C_BEFORE:C_BEFORE + P] = p[:, None] < p[None, :]
    c[:, C_ONES:C_ONES + P] = 1
    c[:, C_SLOT:C_SLOT + P] = p[None, :]
    c[:, C_TILE:C_TILE + TILES] = np.arange(TILES)
    c[:, C_TOKEN:C_TOKEN + TILES] = TILES * p[:, None] + np.arange(TILES)
    c[:, C_UNIT:C_UNIT + UNITS] = np.arange(UNITS)
    c[:, C_PART] = p
    return c


def build(nc, consts, tok, x, ctx_t, ffn_w, scales, down_s, out):
    with ExitStack() as stack:
        def sb(name, shape, dt):
            return stack.enter_context(nc.sbuf_tensor(name, shape, dt))

        def sem(name):
            return stack.enter_context(nc.semaphore(name))

        cst = sb("cst", [P, C_ALL], F32)
        xs = sb("xs", [P, TILES * D], F32)
        ew = sb("ew", [P, EXPERTS * 2 * KD * D], F32R)
        w1 = sb("w1", [P, SLICES * 2 * D], BF16)
        wd = sb("wd", [P, SLICES * D], F32R)
        stage = sb("stage", [P, 2, KD * D], F32)
        xn = sb("xn", [P, 2, D], F32)
        halves = sb("halves", [P, 2, 2, D], F32R)
        gate = sb("gate", [P, D], F32)
        hid = sb("hid", [P, D], F32)
        xt = sb("xt", [P, 4, KD, CHUNK], F16)
        outb = sb("outb", [P, CT, D], F32)
        ds_row = sb("ds_row", [P, D], F32)
        gu_s = sb("gu_s", [P, 2 * SLICES], F32)
        gate_sx = sb("gate_sx", [P, 2 * SLICES], F32)
        tok_sb = sb("tok_sb", [P, TILES], I32)
        ge = sb("ge", [P, EXPERTS - 1, TILES], F32)
        member = sb("member", [P, EXPERTS, TILES], F32)
        zeros = sb("zeros", [P, EXPERTS * TILES], F32)
        upto = sb("upto", [P, EXPERTS * TILES], F32)
        before = sb("before", [P, EXPERTS * TILES], F32)
        rank = sb("rank", [P, EXPERTS, TILES], F32)
        pos_i = sb("pos_i", [P, 3, TILES], I32)
        tile_hot = sb("tile_hot", [P, TILES, TILES], F32)
        tile_tok = sb("tile_tok", [P, TILES, TILES], F16)
        order = sb("order", [P, TILES], I32)
        base = sb("base", [P, EXPERTS], F32)
        edge_i = sb("edge_i", [P, 4, 3], I32)
        edge = sb("edge", [P, 5, 3], F32)
        u_ge = sb("u_ge", [P, 2, 3, UNITS], F32)
        u_red = sb("u_red", [P, 6, UNITS], F32)
        row_ge = sb("row_ge", [P, EXPERTS, UNITS], F32)
        near = sb("near", [P, UNITS + 1, 4], I32)
        unit_expert = sb("unit_expert", [P, UNITS], I32)
        mask = sb("mask", [P, UNITS], F32)
        half_neg = sb("half_neg", [P, CT], F32)
        eps = sb("eps", [P, 1], F32)
        warm = sb("warm", [P, 1], F32)
        bn6 = sb("bn6", [P, CT, 6], F32)
        mv = sb("mv", [P, CT, 2], F32)
        rstd = sb("rstd", [P, 3, CT], F32)
        mv_u = sb("mv_u", [P, 2], F32)
        bn6_u = sb("bn6_u", [P, 6], F32)
        rstd_u = sb("rstd_u", [P, 3], F32)
        inexact = sb("inexact", [P, 2 * SLICES], F32)
        inexact_p = sb("inexact_p", [P, 1], F32)
        general_i = sb("general_i", [P, 1], I32)

        ps = stack.enter_context(nc.psum_tensor("ps", [P, 8, 512], F32))

        cst_in = sem("cst_in")
        tok_in = sem("tok_in")
        scale_in = sem("scale_in")
        expert_in = [sem(f"expert_in{e}") for e in range(EXPERTS)]
        slice_in = sem("slice_in")
        slice_used = sem("slice_used")
        slice_short = sem("slice_short")
        x_in = [sem(f"x_in{q}") for q in range(FIRST + 1)]
        out_done = [sem(f"out_done{t}") for t in range(CT)]
        out_free = sem("out_free")
        again_in = sem("again_in")
        again_used = sem("again_used")
        dve_step = sem("dve_step")
        pool_step = sem("pool_step")
        rest_used = sem("rest_used")
        member_ready = sem("member_ready")
        counts_ready = sem("counts_ready")
        hot_ready = sem("hot_ready")
        order_psum = sem("order_psum")
        order_ready = sem("order_ready")
        units_ready = sem("units_ready")
        half_ready = sem("half_ready")
        expert_high = sem("expert_high")
        expert_low = sem("expert_low")
        count_ready = sem("count_ready")
        count_psum = sem("count_psum")
        general_ready = sem("general_ready")
        u_bn = sem("u_bn")
        bn_seen = sem("bn_seen")
        u_stats = sem("u_stats")
        u_rstd = sem("u_rstd")
        u_norm = sem("u_norm")
        u_xt = sem("u_xt")
        u_xt_high = sem("u_xt_high")
        u_xt_low = sem("u_xt_low")
        u_up = sem("u_up")
        u_silu = sem("u_silu")
        u_hid = sem("u_hid")
        u_ht = sem("u_ht")
        u_ht_high = sem("u_ht_high")
        u_ht_low = sem("u_ht_low")
        u_down = sem("u_down")
        x_now = sem("x_now")
        c_bn = sem("c_bn")
        c_stats = sem("c_stats")
        c_rstd = sem("c_rstd")
        t_norm = sem("t_norm")
        t_xt = sem("t_xt")
        t_high = sem("t_high")
        t_low = sem("t_low")
        s_gate = sem("s_gate")
        s_up = sem("s_up")
        s_silu = sem("s_silu")
        s_hid = sem("s_hid")
        s_high = sem("s_high")
        s_low = sem("s_low")
        s_rest = sem("s_rest")
        s_down = sem("s_down")
        acc_full = sem("acc_full")
        acc_free = sem("acc_free")
        out_ready = sem("out_ready")

        ident = cst[:, C_IDENT:C_IDENT + P]
        slot_hot = xt[:, 0, :, :].rearrange("p k t -> p (k t)").rearrange("p (c s) -> p c s", s=P)
        dump = xt[:, 2, 0:2, :].rearrange("p k t -> p (k t)")
        rest_gu = [stage[:, 1, j * D:(j + 1) * D].bitcast(BF16) for j in range(2)]

        expert_raw = [stage[:, 0, :], stage[:, 1, :], outb[:, :, :].rearrange("p t d -> p (t d)"),
                      w1[:, 0:2 * KD * D].bitcast(F32)]

        def rest_d(i):
            return ew[:, (i % 2) * D:(i % 2 + 1) * D]

        def ew_half(e, part):
            return ew[:, (e * 2 + part) * KD * D:(e * 2 + part + 1) * KD * D]

        def ew_at(e, part, k):
            return ew[:, bass.ds(e * (2 * KD * D) + (part * KD + k) * D, D)]

        def xs_at(q):
            return xs[:, bass.ds(q * D, D)]

        def cols(a, n=P):
            return slice(a * n, (a + 1) * n)

        block = stack.enter_context(nc.Block())

        @block.sync
        def _(sp):
            sp.dma_start(tok_sb[:, :], tok).then_inc(tok_in, 16)
            sp.dma_start(cst[:, :], consts).then_inc(cst_in, 16)
            for e in range(EXPERTS):
                sp.dma_start(expert_raw[e], ctx_t[e]).then_inc(expert_in[e], 16)
            sp.dma_start(gu_s[:, :], scales).then_inc(scale_in, 16)
            sp.dma_start(ds_row[:, :], down_s).then_inc(scale_in, 16)
            sp.wait_ge(expert_low, 2 * 2)
            for s in range(SLICES):
                if s >= 1:
                    sp.wait_ge(slice_in, 16 * s)
                if s >= 2:
                    sp.wait_ge(slice_used, s - 1)
                sp.dma_start(stage[:, s % 2, 0:SLICE_W], ffn_w[s]).then_inc(slice_in, 16)
            sp.wait_ge(general_ready, 1)
            general = sp.value_load(general_i[0:1, 0:1])
            with sp.If(general):
                with sp.Fori(0, CHUNKS) as c:
                    for s in range(SLICES):
                        sp.wait_ge(again_used, c * SLICES + s + 1)
                        sp.dma_start(stage[:, 0, 0:SLICE_W], ffn_w[s]).then_inc(again_in, 16)
            with sp.Else():
                pass

        def chunk_rstd(pool, c):
            pool.wait_ge(c_stats, c + 1)
            pool.tensor_scalar(rstd[:, 0, :], mv[:, :, 1:2].rearrange("p t a -> p (t a)"), EPS, None,
                               ALU.add).then_inc(pool_step, 1)
            pool.wait_ge(pool_step, 2 * UNITS + 2 * c + 1)
            pool.tensor_tensor(rstd[:, 1, :], rstd[:, 0, :], half_neg[:, :], ALU.pow).then_inc(pool_step, 1)
            pool.wait_ge(pool_step, 2 * UNITS + 2 * c + 2)
            pool.tensor_scalar(rstd[:, 2, :], rstd[:, 1, :], XSCALE, None, ALU.mult).then_inc(c_rstd, 1)

        @block.gpsimd
        def _(pool):
            pool.sem_inc(again_used, 1)
            pool.sem_inc(out_free, CT)
            pool.memset(half_neg[:, :], -0.5).then_inc(half_ready, 1)
            pool.memset(eps[:, :], EPS).then_inc(half_ready, 1)
            def unit_rstd(u):
                pool.wait_ge(u_stats, u + 1)
                pool.tensor_tensor(rstd_u[:, 0:1], mv_u[:, 1:2], eps[:, :], ALU.add).then_inc(pool_step, 1)
                pool.wait_ge(pool_step, 2 * u + 1)
                pool.tensor_tensor(rstd_u[:, 1:2], rstd_u[:, 0:1], half_neg[:, 0:1], ALU.pow).then_inc(pool_step, 1)
                pool.wait_ge(pool_step, 2 * u + 2)
                pool.tensor_tensor(rstd_u[:, 2:3], rstd_u[:, 1:2], mask[:, bass.ds(u, 1)],
                                   ALU.mult).then_inc(u_rstd, 1)

            pool.wait_ge(order_ready, 1)
            factor_after = {4: 0, 7: 1, 10: 2}
            for q in range(TILES):
                pool.indirect_dma_start(
                    xs[:, q * D:(q + 1) * D], None, x,
                    bass.IndirectOffsetOnAxis(ap=order[:, q:q + 1], axis=0)).then_inc(x_in[min(q, FIRST)], 16)
                if q in factor_after:
                    pool.wait_ge(units_ready, 1)
                    unit_rstd(factor_after[q])
            with pool.Fori(FIRST, UNITS) as u:
                unit_rstd(u)
            for c in range(CHUNKS):
                if c == 0:
                    chunk_rstd(pool, 0)
                if c + 1 < CHUNKS:
                    chunk_rstd(pool, c + 1)
                for t in range(CT):
                    q = c * CT + t
                    pool.wait_ge(out_ready, q + 1)
                    pool.indirect_dma_start(
                        out, bass.IndirectOffsetOnAxis(ap=order[:, q:q + 1], axis=0),
                        outb[:, t, :], None).then_inc(out_done[t], 16)
                for t in range(CT):
                    pool.wait_ge(out_done[t], 16 * c + 16)
                    pool.sem_inc(out_free, 1)

        @block.scalar
        def _(act):
            act.wait_ge(half_ready, 2)
            act.activation(warm[:, :], half_neg[:, 0:1], ACT.Silu)
            for e in range(EXPERTS):
                act.wait_ge(expert_in[e], 16)
                act.activation(ew_half(e, 0), expert_raw[e], ACT.Copy).then_inc(expert_high, 1)

            def xt_high(u):
                act.wait_ge(u_xt, u + 1)
                act.activation(halves[:, 0, 0, :], ps[:, B_UX, :], ACT.Copy).then_inc(u_xt_high, 1)

            def silu(u):
                act.wait_ge(u_up, u + 1)
                act.activation(gate[:, :], ps[:, B_G, :], ACT.Silu).then_inc(u_silu, 1)

            def ht_high(u):
                act.wait_ge(u_ht, u + 1)
                act.activation(halves[:, 1, 0, :], ps[:, B_HT, :], ACT.Copy).then_inc(u_ht_high, 1)

            def shorten(s):
                act.wait_ge(slice_in, 16 * s + 16)
                act.activation(w1[:, bass.ds(s * (2 * D), 2 * D)],
                               stage[:, bass.ds(s % 2, 1), 0:2 * D].rearrange("p a w -> p (a w)"),
                               ACT.Copy).then_inc(slice_short, 1)
                act.activation(wd[:, bass.ds(s * D, D)],
                               stage[:, bass.ds(s % 2, 1), 2 * D:3 * D].rearrange("p a w -> p (a w)"),
                               ACT.Copy).then_inc(slice_short, 1)

            xt_high(0)
            silu(0)
            xt_high(1)
            with act.Fori(1, SLICES + 1) as u:
                ht_high(u - 1)
                shorten(u - 1)
                silu(u)
                xt_high(u + 1)
            with act.Fori(SLICES + 1, UNITS - 1) as u:
                ht_high(u - 1)
                silu(u)
                xt_high(u + 1)

            def tile_high(t, slot, tt):
                act.wait_ge(t_xt, t + 1)
                act.activation(xt[:, bass.ds(2 * slot, 1), :, cols(tt)].rearrange("p a k t -> p (a k) t"),
                               ps[:, B_XT + tt % 2, :].rearrange("p (k t) -> p k t", k=KD),
                               ACT.Copy).then_inc(t_high, 1)

            ht_high(UNITS - 2)
            silu(UNITS - 1)
            tile_high(0, 0, 0)
            tile_high(1, 0, 1)
            ht_high(UNITS - 1)
            for t in range(2, CT):
                tile_high(t, 0, t)

            def chunk(c, last):
                for i in range(SLICES):
                    n = c * SLICES + i
                    act.wait_ge(s_gate, n + 1)
                    if i >= 1:
                        act.wait_ge(s_hid, n)
                    act.activation(gate[:, :], ps[:, B_G, :], ACT.Silu, scale=gate_sx[:, i:i + 1]).then_inc(s_silu, 1)
                    act.wait_ge(s_hid, n + 1)
                    act.activation(halves[:, i % 2, 0, :], hid[:, :], ACT.Copy).then_inc(s_high, 1)
                    if not last and i in TURN_AT:
                        t = TURN_AT.index(i)
                        tile_high(c * CT + CT + t, (c + 1) % 2, t)

            with act.Fori(0, CHUNKS - 1) as c:
                chunk(c, False)
            chunk(CHUNKS - 1, True)

        @block.vector
        def _(dve):
            steps = [0]

            def step(ins):
                steps[0] += 1
                ins.then_inc(dve_step, 1)
                dve.wait_ge(dve_step, steps[0])

            dve.memset(zeros[:, :], 0.0)
            dve.memset(base[:, 3:4], float(TOKENS))
            dve.memset(near[0:1, :, :], 0)
            dve.wait_ge(tok_in, 16)
            for e in range(1, EXPERTS):
                last = dve.tensor_scalar(ge[:, e - 1, :], tok_sb[:, :], float(e * PER_EXPERT), None, ALU.is_ge)
            step(last)
            dve.tensor_scalar(member[:, 0, :], ge[:, 0, :], -1.0, 1.0, ALU.mult, ALU.add)
            dve.tensor_tensor(member[:, 1:3, :], ge[:, 0:2, :], ge[:, 1:3, :], ALU.subtract)
            dve.tensor_copy(member[:, 3, :], ge[:, 2, :]).then_inc(member_ready, 1)
            dve.wait_ge(counts_ready, 1)
            totals = ps[:, B_ACC + 2, 0:EXPERTS * TILES]
            earlier = ps[:, B_ACC + 2, P:P + EXPERTS * TILES]
            step(dve.tensor_tensor_scan(upto[:, :], totals, zeros[:, :], 0.0, ALU.add, ALU.add))
            step(dve.tensor_tensor(before[:, :], upto[:, :], totals, ALU.subtract))
            step(dve.tensor_tensor(rank[:, :, :].rearrange("p e c -> p (e c)"), earlier, before[:, :], ALU.add))
            step(dve.tensor_tensor(rank[:, :, :], rank[:, :, :], member[:, :, :], ALU.mult))
            with nc.allow_low_precision(reason="whole numbers below TOKENS"):
                step(dve.tensor_reduce(pos_i[:, 0, :], rank[:, :, :].rearrange("p e c -> p c e"), AX, ALU.add))
            dve.tensor_scalar(pos_i[:, 2, :], pos_i[:, 0, :], 7, None, ALU.logical_shift_right)
            step(dve.tensor_scalar(pos_i[:, 1, :], pos_i[:, 0, :], P - 1, None, ALU.bitwise_and))
            dve.wait_ge(cst_in, 16)
            step(dve.tensor_tensor(tile_hot[:, :, :], pos_i[:, 2, :].unsqueeze(2).broadcast_to([P, TILES, TILES]),
                                   cst[:, C_TILE:C_TILE + TILES].unsqueeze(1).broadcast_to([P, TILES, TILES]),
                                   ALU.is_equal))
            dve.tensor_tensor(tile_tok[:, :, :], tile_hot[:, :, :],
                              cst[:, C_TOKEN:C_TOKEN + TILES].unsqueeze(2).broadcast_to([P, TILES, TILES]),
                              ALU.mult)
            dve.tensor_tensor(slot_hot, pos_i[:, 1, :].unsqueeze(2).broadcast_to([P, TILES, P]),
                              cst[:, C_SLOT:C_SLOT + P].unsqueeze(1).broadcast_to([P, TILES, P]),
                              ALU.is_equal).then_inc(hot_ready, 1)
            dve.tensor_copy(base[:, 0:3], before[:, TILES::TILES])
            dve.tensor_scalar(edge_i[:, 1, :], before[:, TILES::TILES], float(P - 1), None, ALU.add)
            step(dve.tensor_copy(edge_i[:, 0, :], before[:, TILES::TILES]))
            step(dve.tensor_scalar(edge_i[:, 2:4, :], edge_i[:, 0:2, :], 7, None, ALU.logical_shift_right))
            step(dve.tensor_copy(edge[:, 0:2, :], edge_i[:, 2:4, :]))
            step(dve.tensor_tensor(edge[:, 2, :], edge[:, 0, :], edge[:, 1, :], ALU.subtract))
            step(dve.tensor_tensor_scan(edge[:, 3, :], edge[:, 2, :], zeros[:, 0:3], 0.0, ALU.add, ALU.add))
            step(dve.tensor_tensor(edge[:, 3, :], edge[:, 3, :], edge[:, 2, :], ALU.subtract))
            step(dve.tensor_tensor(edge[:, 4, :], edge[:, 1, :], edge[:, 3, :], ALU.subtract))

            dve.wait_ge(order_psum, 1)
            dve.tensor_copy(order[:, :], ps[:, B_ACC + 3, 0:TILES]).then_inc(order_ready, 1)

            unit_row = cst[:, C_UNIT:C_UNIT + UNITS]
            step(dve.tensor_tensor(u_ge[:, 0, :, :], unit_row.unsqueeze(1).broadcast_to([P, 3, UNITS]),
                                   edge[:, 4, :].unsqueeze(2).broadcast_to([P, 3, UNITS]), ALU.is_ge))
            step(dve.tensor_tensor(u_ge[:, 1, :, :], u_ge[:, 0, :, :],
                                   edge[:, 2, :].unsqueeze(2).broadcast_to([P, 3, UNITS]), ALU.mult))
            dve.tensor_reduce(u_red[:, 0, :], u_ge[:, 0, :, :].rearrange("p e u -> p u e"), AX, ALU.add)
            step(dve.tensor_reduce(u_red[:, 1, :], u_ge[:, 1, :, :].rearrange("p e u -> p u e"), AX, ALU.add))
            step(dve.tensor_tensor(u_red[:, 2, :], u_red[:, 1, :], unit_row, ALU.add))
            step(dve.tensor_scalar(u_red[:, 3, :], u_red[:, 2, :], float(P), cst[:, C_PART:C_PART + 1],
                                   ALU.mult, ALU.add))
            step(dve.tensor_tensor(row_ge[:, :, :], u_red[:, 3, :].unsqueeze(1).broadcast_to([P, EXPERTS, UNITS]),
                                   base[:, :].unsqueeze(2).broadcast_to([P, EXPERTS, UNITS]), ALU.is_ge))
            step(dve.tensor_reduce(u_red[:, 4, :], row_ge[:, :, :].rearrange("p e u -> p u e"), AX, ALU.add))
            step(dve.tensor_tensor(mask[:, :], u_red[:, 4, :], u_red[:, 0, :], ALU.is_equal))
            step(dve.tensor_scalar(u_red[:, 5, :], u_red[:, 2, :], float(TILES - 1), None, ALU.min))
            dve.tensor_copy(near[0:1, 1:UNITS + 1, 0], u_red[0:1, 5, :])
            dve.tensor_copy(near[0:1, 0:UNITS - 2, 1], u_red[0:1, 5, 2:UNITS])
            dve.tensor_copy(near[0:1, 0:UNITS - 3, 2], u_red[0:1, 5, 3:UNITS])
            dve.tensor_copy(unit_expert[0:1, :], u_red[0:1, 0, :]).then_inc(units_ready, 1)
            dve.wait_ge(units_ready, 1)

            def expert_rest(e, part):
                half = slice(part * KD * D // 2, (part + 1) * KD * D // 2)
                dve.wait_ge(expert_high, e + 1)
                dve.tensor_tensor(ew_half(e, 1)[:, half], expert_raw[e][:, half],
                                  ew_half(e, 0)[:, half].bitcast(F32), ALU.subtract).then_inc(expert_low, 1)

            def tiles_near(u):
                _, q = nc.values_load_multi_w_load_instructions(
                    near[0:1, bass.ds(u, 1), 0:3].rearrange("p a q -> p (a q)"),
                    engines=(mybir.EngineType.DVE,), min_val=0, max_val=TILES - 1)
                return q

            def stats(u, q):
                dve.wait_ge(x_in[FIRST], 16 * (TILES - FIRST))
                dve.wait_ge(u_norm, u)
                dve.bn_stats(bn6_u[:, :], xs_at(q)).then_inc(u_bn, 1)
                dve.wait_ge(u_bn, u + 1)
                dve.sem_inc(bn_seen, 1)
                dve.bn_aggr(mv_u[:, :], bn6_u[:, :]).then_inc(u_stats, 1)

            def stats_first(u):
                q = 0 if u == 0 else dve.value_load(near[0:1, u + 1, 0:1], min_val=0, max_val=u)
                dve.wait_ge(x_in[u], 16)
                if u >= 1:
                    dve.wait_ge(u_norm, u)
                dve.bn_stats(bn6_u[:, :], xs_at(q)).then_inc(u_bn, 1)
                dve.wait_ge(u_bn, u + 1)
                dve.bn_aggr(mv_u[:, :], bn6_u[:, :]).then_inc(u_stats, 1)
                return q

            def norm(u, q):
                dve.wait_ge(u_rstd, u + 1)
                dve.tensor_scalar(xn[:, 0, :], xs_at(q), mv_u[:, 0:1], rstd_u[:, 2:3],
                                  ALU.subtract, ALU.mult).then_inc(u_norm, 1)

            def xt_low(u):
                dve.wait_ge(u_xt_high, u + 1)
                dve.tensor_tensor(halves[:, 0, 1, :], ps[:, B_UX, :], halves[:, 0, 0, :].bitcast(F32),
                                  ALU.subtract).then_inc(u_xt_low, 1)

            def hidden(u):
                dve.wait_ge(u_silu, u + 1)
                dve.tensor_tensor(hid[:, :], ps[:, B_G, :], gate[:, :], ALU.mult).then_inc(u_hid, 1)

            def ht_low(u):
                dve.wait_ge(u_ht_high, u + 1)
                dve.tensor_tensor(halves[:, 1, 1, :], ps[:, B_HT, :], halves[:, 1, 0, :].bitcast(F32),
                                  ALU.subtract).then_inc(u_ht_low, 1)

            def add(u, q):
                dve.wait_ge(u_down, u + 1)
                dve.tensor_tensor(xs_at(q), ps[:, B_U, :], xs_at(q), ALU.add).then_inc(x_now, 1)

            def compare(s, part):
                raw = stage[:, bass.ds(s % 2, 1), 0:SLICE_W].rearrange("p a w -> p (a w)")
                if part == 0:
                    dve.wait_ge(slice_short, 2 * s + 2)
                    dve.scalar_tensor_tensor(dump, raw[:, 0:2 * D], 1.0, w1[:, bass.ds(s * (2 * D), 2 * D)],
                                             ALU.mult, ALU.not_equal,
                                             accum_out=inexact[:, bass.ds(2 * s, 1)]).then_inc(count_ready, 1)
                    return
                dve.wait_ge(count_ready, 2 * s + 1)
                dve.scalar_tensor_tensor(dump[:, 0:D], raw[:, 2 * D:3 * D], 1.0,
                                         wd[:, bass.ds(s * D, D)].bitcast(F32), ALU.mult, ALU.not_equal,
                                         accum_out=inexact[:, bass.ds(2 * s + 1, 1)]).then_inc(count_ready, 1)

            def unit(u, norms, statistics, checks):
                q = tiles_near(u)
                hidden(u)
                xt_low(u + 1)
                if checks:
                    compare(u - 1, 0)
                    compare(u - 1, 1)
                add(u - 1, q[0])
                if checks:
                    dve.wait_ge(count_ready, 2 * u)
                    dve.sem_inc(slice_used, 1)
                if norms:
                    dve.wait_ge(x_now, u + 1)
                    norm(u + 2, q[1])
                ht_low(u)
                if statistics:
                    stats(u + 3, q[2])

            expert_rest(0, 0)
            expert_rest(0, 1)
            q = stats_first(0)
            expert_rest(1, 0)
            norm(0, q)
            expert_rest(1, 1)
            q = stats_first(1)
            xt_low(0)
            dve.wait_ge(u_xt, 1)
            norm(1, q)
            dve.wait_ge(scale_in, 32)
            dve.tensor_scalar(gate_sx[:, :], gu_s[:, :], 1.0 / XSCALE, None, ALU.mult).then_inc(x_now, 1)
            for e in (2, 3):
                expert_rest(e, 0)
                expert_rest(e, 1)
            q = stats_first(2)
            hidden(0)
            xt_low(1)
            norm(2, q)
            ht_low(0)
            q = dve.value_load(near[0:1, 4, 0:1], min_val=0, max_val=3)
            stats(3, q)
            with dve.Fori(1, SLICES + 1) as u:
                unit(u, True, True, True)
            with dve.Fori(SLICES + 1, UNITS - 3) as u:
                unit(u, True, True, False)
            unit(UNITS - 3, True, False, False)
            unit(UNITS - 2, False, False, False)
            dve.tensor_reduce(inexact_p[:, :], inexact[:, :], AX, ALU.add).then_inc(count_ready, 1)

            def chunk_stats(c, t):
                dve.bn_stats(bn6[:, t, :], xs_at(c * CT + t)).then_inc(c_bn, 1)

            def chunk_aggr(t):
                ins = dve.bn_aggr(mv[:, t, :], bn6[:, t, :])
                if t == CT - 1:
                    ins.then_inc(c_stats, 1)

            def tile_norm(c, t):
                n = c * CT + t
                dve.wait_ge(c_rstd, c + 1)
                dve.tensor_scalar(xn[:, t % 2, :], xs_at(n), mv[:, t, 0:1], rstd[:, 2, t:t + 1],
                                  ALU.subtract, ALU.mult).then_inc(t_norm, 1)

            def tile_low(c, slot, t):
                n = c * CT + t
                dve.wait_ge(t_high, n + 1)
                dve.tensor_tensor(xt[:, bass.ds(2 * slot + 1, 1), :, cols(t)].rearrange("p a k t -> p (a k) t"),
                                  ps[:, B_XT + t % 2, :].rearrange("p (k t) -> p k t", k=KD),
                                  xt[:, bass.ds(2 * slot, 1), :, cols(t)].rearrange("p a k t -> p (a k) t"),
                                  ALU.subtract).then_inc(t_low, 1)

            dve.wait_ge(x_now, UNITS - 1)
            for t in range(CT):
                chunk_stats(0, t)
            dve.wait_ge(c_bn, CT)
            for t in range(CT):
                chunk_aggr(t)
            q_last = dve.value_load(near[0:1, UNITS, 0:1], min_val=0, max_val=TILES - 1)
            q_before = dve.value_load(near[0:1, UNITS - 1, 0:1], min_val=0, max_val=TILES - 1)
            dve.wait_ge(u_xt, UNITS)
            tile_norm(0, 0)
            tile_norm(0, 1)
            hidden(UNITS - 1)
            tile_low(0, 0, 0)
            dve.wait_ge(t_xt, 1)
            tile_norm(0, 2)
            add(UNITS - 2, q_before)
            ht_low(UNITS - 1)
            tile_low(0, 0, 1)
            dve.wait_ge(t_xt, 2)
            tile_norm(0, 3)
            dve.wait_ge(count_psum, 1)
            dve.tensor_copy(general_i[0:1, 0:1], ps[0:1, B_ACC + 3, 0:1]).then_inc(general_ready, 1)
            tile_low(0, 0, 2)
            tile_low(0, 0, 3)
            dve.wait_ge(x_now, UNITS)
            add(UNITS - 1, q_last)
            dve.wait_ge(x_now, UNITS + 1)
            dve.sem_inc(acc_free, 1)
            dve.wait_ge(general_ready, 1)
            general = dve.value_load(general_i[0:1, 0:1])

            def remainders(c, i):
                n = c * SLICES + i
                raw_gu, raw_d = stage[:, 0, 0:2 * D], stage[:, 0, 2 * D:3 * D]
                dve.wait_ge(again_in, 16 * n + 16)
                if i >= 2:
                    dve.wait_ge(s_down, c * (SLICES - 1) + i - 1)
                if i >= 1:
                    dve.wait_ge(s_up, n)
                dve.tensor_tensor(raw_gu, raw_gu, w1[:, i * 2 * D:(i + 1) * 2 * D],
                                  ALU.subtract).then_inc(rest_used, 1)
                dve.wait_ge(rest_used, 2 * n + 1)
                dve.tensor_copy(rest_gu[0], raw_gu).then_inc(rest_used, 1)
                dve.wait_ge(rest_used, 2 * n + 2)
                dve.tensor_tensor(rest_gu[1], raw_gu, rest_gu[0], ALU.subtract)
                dve.tensor_tensor(rest_d(i), raw_d, wd[:, i * D:(i + 1) * D].bitcast(F32),
                                  ALU.subtract).then_inc(s_rest, 1)
                dve.wait_ge(s_rest, n + 1)
                dve.sem_inc(again_used, 1)

            def chunk(c, last, rest):
                for i in range(SLICES):
                    n = c * SLICES + i
                    if rest:
                        remainders(c, i)
                    if not last and i == 1:
                        dve.wait_ge(c_bn, CT * c + 2 * CT)
                    if i >= 1:
                        dve.wait_ge(s_low, n)
                    dve.wait_ge(s_up, n + 1)
                    dve.wait_ge(s_silu, n + 1)
                    dve.scalar_tensor_tensor(hid[:, :], ps[:, B_U, :], gate_sx[:, SLICES + i:SLICES + i + 1],
                                             gate[:, :], ALU.mult, ALU.mult).then_inc(s_hid, 1)
                    if not last and i == 1:
                        for t in range(CT):
                            chunk_aggr(t)
                    dve.wait_ge(s_high, n + 1)
                    dve.tensor_tensor(halves[:, i % 2, 1, :], hid[:, :], halves[:, i % 2, 0, :].bitcast(F32),
                                      ALU.subtract).then_inc(s_low, 1)
                    if not last and i == 0:
                        for t in range(CT):
                            chunk_stats(c + 1, t)
                    if not last and i in TURN_AT:
                        tile_low(c + 1, (c + 1) % 2, TURN_AT.index(i))
                    if not last and i in NORM_AT:
                        t = NORM_AT.index(i)
                        dve.wait_ge(t_xt, c * CT + CT + t - 1)
                        tile_norm(c + 1, t)

                def scale_out(t):
                    dve.wait_ge(acc_full, c * CT + t + 1)
                    dve.wait_ge(out_free, c * CT + t + 1)
                    dve.tensor_tensor(outb[:, t, :], ps[:, B_ACC + t, :], ds_row[:, :],
                                      ALU.mult).then_inc(acc_free, 1)

                def sum_out(t):
                    dve.wait_ge(acc_free, c * CT + t + 2)
                    dve.tensor_tensor(outb[:, t, :], outb[:, t, :], xs_at(c * CT + t),
                                      ALU.add).then_inc(out_ready, 1)

                for t in range(CT):
                    scale_out(t)
                    if t >= 1:
                        sum_out(t - 1)
                sum_out(CT - 1)

            def dense(rest):
                with dve.Fori(0, CHUNKS - 1) as c:
                    chunk(c, False, rest)
                chunk(CHUNKS - 1, True, rest)

            with dve.If(general):
                dense(True)
            with dve.Else():
                dense(False)

        @block.tensor
        def _(pe):
            pe.wait_ge(cst_in, 16)
            pe.wait_ge(member_ready, 1)
            members = member[:, :, :].rearrange("p e c -> p (e c)")
            n_cols = EXPERTS * TILES
            pe.matmul(ps[:, B_ACC + 2, 0:n_cols], cst[:, C_ONES:C_ONES + P], members, start=True, stop=True)
            pe.matmul(ps[:, B_ACC + 2, P:P + n_cols], cst[:, C_BEFORE:C_BEFORE + P], members,
                      start=True, stop=True).then_inc(counts_ready, 1)
            pe.wait_ge(hot_ready, 1)
            for c in range(TILES):
                mm = pe.matmul(ps[:, B_ACC + 3, 0:TILES], slot_hot[:, c, :], tile_tok[:, c, :],
                               start=(c == 0), stop=(c == TILES - 1))
            mm.then_inc(order_psum, 1)
            pe.wait_ge(units_ready, 1)

            def expert_of(u):
                return pe.value_load(unit_expert[0:1, bass.ds(u, 1)], min_val=0, max_val=EXPERTS - 1)

            def split_product(dst, slot, e):
                passes = [(k, a, b) for k in range(KD) for a, b in ((0, 0), (0, 1), (1, 0))]
                for n, (k, a, b) in enumerate(passes):
                    mm = pe.matmul(dst, halves[:, slot, a, cols(k)], ew_at(e, b, k),
                                   start=(n == 0), stop=(n == len(passes) - 1))
                return mm

            def turn(bank, src):
                for k in range(KD):
                    mm = pe.transpose(ps[:, bank, cols(k)], src[:, cols(k)], ident)
                return mm

            def turn_x(u):
                pe.wait_ge(u_norm, u + 1)
                turn(B_UX, xn[:, 0, :]).then_inc(u_xt, 1)

            def up(u):
                pe.wait_ge(u_xt_low, u + 1)
                e = expert_of(u)
                if isinstance(u, int) and u == 0:
                    pe.wait_ge(expert_low, 2 * e + 2)
                split_product(ps[:, B_G, :], 0, e).then_inc(u_up, 1)

            def turn_h(u):
                pe.wait_ge(u_hid, u + 1)
                turn(B_HT, hid).then_inc(u_ht, 1)

            def down(u):
                pe.wait_ge(u_ht_low, u + 1)
                pe.wait_ge(x_now, u + 1)
                split_product(ps[:, B_U, :], 1, expert_of(u)).then_inc(u_down, 1)

            turn_x(0)
            up(0)
            turn_x(1)
            turn_h(0)
            with pe.Fori(1, UNITS - 1) as u:
                up(u)
                turn_x(u + 1)
                down(u - 1)
                turn_h(u)

            def turn_tile(t, tt):
                pe.wait_ge(t_norm, t + 1)
                turn(B_XT + tt % 2, xn[:, tt % 2, :]).then_inc(t_xt, 1)

            up(UNITS - 1)
            turn_tile(0, 0)
            turn_tile(1, 1)
            down(UNITS - 2)
            turn_h(UNITS - 1)
            pe.wait_ge(count_ready, 2 * SLICES + 1)
            pe.matmul(ps[:, B_ACC + 3, 0:1], cst[:, C_ONES:C_ONES + P], inexact_p[:, :],
                      start=True, stop=True).then_inc(count_psum, 1)
            for t in range(2, CT):
                pe.wait_ge(t_low, t - 1)
                turn_tile(t, t)
            down(UNITS - 1)
            pe.wait_ge(general_ready, 1)
            general = pe.value_load(general_i[0:1, 0:1])

            def gate_or_up(bank, i, which, slot, rest):
                at = (i * 2 + which) * D
                parts = []
                for k in range(KD):
                    parts += [(w1[:, at + k * P:at + (k + 1) * P], 0, k), (w1[:, at + k * P:at + (k + 1) * P], 1, k)]
                    if rest:
                        r = [rest_gu[j][:, which * D + k * P:which * D + (k + 1) * P] for j in range(2)]
                        parts += [(r[0], 0, k), (r[0], 1, k), (r[1], 0, k)]
                for n, (w, part, k) in enumerate(parts):
                    mm = pe.matmul(ps[:, bank, :], w,
                                   xt[:, bass.ds(2 * slot + part, 1), k, :].rearrange("p a t -> p (a t)"),
                                   start=(n == 0), stop=(n == len(parts) - 1))
                return mm

            def slice_down(c, i, rest):
                n = c * SLICES + i
                pe.wait_ge(s_low, n + 1)
                if i == 0:
                    pe.wait_ge(acc_free, c * CT + 1)
                for t in range(CT):
                    rhs = wd[:, i * D:(i + 1) * D]
                    pairs = [(0, rhs), (1, rhs)]
                    if rest:
                        pairs += [(0, rest_d(i)), (1, rest_d(i))]
                    for m, (part, r) in enumerate(pairs):
                        mm = pe.matmul(ps[:, B_ACC + t, :], halves[:, i % 2, part, cols(t)], r,
                                       start=(i == 0 and m == 0), stop=(i == SLICES - 1 and m == len(pairs) - 1))
                    if i == SLICES - 1:
                        mm.then_inc(acc_full, 1)
                if rest and i < SLICES - 1:
                    mm.then_inc(s_down, 1)

            def chunk(c, last, rest):
                slot = c % 2
                for i in range(SLICES):
                    n = c * SLICES + i
                    if i == 0:
                        pe.wait_ge(t_low, c * CT + CT)
                    else:
                        pe.wait_ge(s_silu, n)
                    if rest:
                        pe.wait_ge(s_rest, n + 1)
                    gate_or_up(B_G, i, 0, slot, rest).then_inc(s_gate, 1)
                    if i >= 1:
                        pe.wait_ge(s_hid, n)
                    elif not isinstance(c, int) or c == 0:
                        pe.wait_ge(x_now, UNITS + 1)
                    gate_or_up(B_U, i, 1, slot, rest).then_inc(s_up, 1)
                    if i >= 1:
                        slice_down(c, i - 1, rest)
                    if not last and i in TURN_AT:
                        t = TURN_AT.index(i)
                        pe.wait_ge(t_low, c * CT + CT + t - 1)
                        turn_tile(c * CT + CT + t, t)
                slice_down(c, SLICES - 1, rest)

            def dense(rest):
                with pe.Fori(0, CHUNKS - 1) as c:
                    chunk(c, False, rest)
                chunk(CHUNKS - 1, True, rest)

            with pe.If(general):
                dense(True)
            with pe.Else():
                dense(False)


def kernel(x, itok_BxS_13_99985, ctx_2048, L0_ffn_gate_w, L0_ffn_up_w, L0_ffn_down_w,
           L0_ffn_gate_s, L0_ffn_up_s, L0_ffn_down_s):
    import concourse.bacc as bacc
    from concourse.bass_utils import run_bass_kernel_spmd

    x = np.asarray(x)
    shape = x.shape

    def by_slice(w):
        return np.asarray(w).reshape(SLICES, P, KD, P).transpose(0, 3, 2, 1).reshape(SLICES, P, D)

    down = np.asarray(L0_ffn_down_w).T.reshape(SLICES, P, D)
    arrays = {
        "consts": constants(),
        "tok": np.asarray(itok_BxS_13_99985).reshape(P, TILES),
        "x_rows": x.reshape(TOKENS, D),
        "ctx_t": np.asarray(ctx_2048).transpose(0, 2, 1).reshape(EXPERTS, KD, P, D)
                   .transpose(0, 2, 1, 3).reshape(EXPERTS, P, KD * D),
        "ffn_w": np.concatenate([by_slice(L0_ffn_gate_w), by_slice(L0_ffn_up_w), down], axis=2),
        "scales": np.concatenate([np.asarray(L0_ffn_gate_s).reshape(SLICES, P).T,
                                  np.asarray(L0_ffn_up_s).reshape(SLICES, P).T], axis=1),
        "down_s": np.broadcast_to(np.asarray(L0_ffn_down_s)[None, :], (P, D)),
    }
    arrays = {k: np.ascontiguousarray(a) for k, a in arrays.items()}
    nc = bacc.Bacc("TRN2", target_bir_lowering=False, num_devices=1)
    args = [nc.dram_tensor(k, a.shape, mybir.dt.from_np(a.dtype), kind="ExternalInput").ap()
            for k, a in arrays.items()]
    res = nc.dram_tensor("y_rows", (TOKENS, D), F32, kind="ExternalOutput").ap()
    build(nc, *args, res)
    r = run_bass_kernel_spmd(nc, [arrays], core_ids=[0])
    return r.results[0]["y_rows"].reshape(shape)
```

```python
from contextlib import ExitStack

import numpy as np
import concourse.bass as bass
from concourse import mybir

F32 = mybir.dt.float32
F32R = mybir.dt.float32r
F16 = mybir.dt.float16
BF16 = mybir.dt.bfloat16
I32 = mybir.dt.int32
ALU = mybir.AluOpType
ACT = mybir.ActivationFunctionType
AX = mybir.AxisListType.X

P = 128
D = 512
KD = D // P
TOKENS = 2048
TILES = TOKENS // P
EXPERTS = 4
VOCAB = 25000
PER_EXPERT = VOCAB // EXPERTS
UNITS = TILES + EXPERTS - 1
INTER = 1408
SLICES = INTER // P
SLICE_W = 3 * D
CHUNK = 512
CT = CHUNK // P
CHUNKS = TOKENS // CHUNK
TURN_AT = [3, 5, 10, 10]
NORM_AT = [2, 4, 6, 8]
WARM_UP = 20
EARLY = 6
FACTOR_AFTER = [3, 5, 8, 10, 13]
EARLY_UNITS = len(FACTOR_AFTER)
EPS = 1e-5
XSCALE = 256.0

C_BEFORE, C_ONES, C_IDENT, C_SLOT = 0, P, 2 * P, 3 * P
C_TILE = 4 * P
C_TOKEN = C_TILE + TILES
C_UNIT = C_TOKEN + TILES
C_PART = C_UNIT + UNITS
C_ALL = C_PART + 1

HALF = CHUNK // 2
B_G, B_U = 0, 1
B_ACC, B_XT = 2, 6
FIRST_XT = [6, 7, 3, 4]
HALF_BANKS = [(0, 1), (6, 7)]
B_HT, B_UX = 2, 3


def constants():
    c = np.zeros((P, C_ALL), np.float32)
    p = np.arange(P)
    c[:, C_IDENT:C_IDENT + P] = np.eye(P)
    c[:, C_BEFORE:C_BEFORE + P] = p[:, None] < p[None, :]
    c[:, C_ONES:C_ONES + P] = 1
    c[:, C_SLOT:C_SLOT + P] = p[None, :]
    c[:, C_TILE:C_TILE + TILES] = np.arange(TILES)
    c[:, C_TOKEN:C_TOKEN + TILES] = TILES * p[:, None] + np.arange(TILES)
    c[:, C_UNIT:C_UNIT + UNITS] = np.arange(UNITS)
    c[:, C_PART] = p
    return c


def build(nc, consts, tok, x, ctx_t, ffn_w, scales, down_s, out):
    with ExitStack() as stack:
        def sb(name, shape, dt):
            return stack.enter_context(nc.sbuf_tensor(name, shape, dt))

        def sem(name):
            return stack.enter_context(nc.semaphore(name))

        cst = sb("cst", [P, C_ALL], F32)
        xs = sb("xs", [P, TILES * D], F32)
        ew = sb("ew", [P, EXPERTS * 2 * KD * D], F32R)
        w1 = sb("w1", [P, SLICES * 2 * D], BF16)
        wd = sb("wd", [P, SLICES * D], F32R)
        stage = sb("stage", [P, 2, KD * D], F32)
        xn = sb("xn", [P, 2, D], F32)
        halves = sb("halves", [P, 2, 2, D], F32R)
        gate = sb("gate", [P, D], F32)
        hid = sb("hid", [P, D], F32)
        xt = sb("xt", [P, 4, KD, CHUNK], F16)
        outb = sb("outb", [P, CT, D], F32)
        ds_row = sb("ds_row", [P, D], F32)
        gu_s = sb("gu_s", [P, 2 * SLICES], F32)
        gate_sx = sb("gate_sx", [P, 2 * SLICES], F32)
        tok_sb = sb("tok_sb", [P, TILES], I32)
        ge = sb("ge", [P, EXPERTS - 1, TILES], F32)
        member = sb("member", [P, EXPERTS, TILES], F32)
        zeros = sb("zeros", [P, EXPERTS * TILES], F32)
        upto = sb("upto", [P, EXPERTS * TILES], F32)
        before = sb("before", [P, EXPERTS * TILES], F32)
        rank = sb("rank", [P, EXPERTS, TILES], F32)
        pos_i = sb("pos_i", [P, 3, TILES], I32)
        tile_hot = sb("tile_hot", [P, TILES, TILES], F32)
        tile_tok = sb("tile_tok", [P, TILES, TILES], F16)
        order = sb("order", [P, TILES], I32)
        base = sb("base", [P, EXPERTS], F32)
        first_i = sb("first_i", [P, 2, 3], I32)
        first_unit = sb("first_unit", [P, 3], F32)
        u_ge = sb("u_ge", [P, 3, UNITS], F32)
        u_expert = sb("u_expert", [P, UNITS], F32)
        u_tile = sb("u_tile", [P, 2, UNITS], F32)
        u_row = sb("u_row", [P, UNITS], F32)
        row_expert = sb("row_expert", [P, UNITS], F32)
        row_ge = sb("row_ge", [P, EXPERTS, UNITS], F32)
        near = sb("near", [P, UNITS + 1, 4], I32)
        unit_expert = sb("unit_expert", [P, UNITS], I32)
        mask = sb("mask", [P, UNITS], F32)
        half_neg = sb("half_neg", [P, CT], F32)
        eps = sb("eps", [P, 1], F32)
        warm = sb("warm", [P, 1], F32)
        bn6 = sb("bn6", [P, CT, 6], F32)
        mv = sb("mv", [P, CT, 2], F32)
        rstd = sb("rstd", [P, 3, CT], F32)
        mv_u = sb("mv_u", [P, 2], F32)
        bn6_u = sb("bn6_u", [P, 6], F32)
        rstd_u = sb("rstd_u", [P, 3], F32)
        inexact = sb("inexact", [P, SLICES], F32)
        inexact_p = sb("inexact_p", [P, 2], F32)
        general_i = sb("general_i", [P, 1], I32)

        ps = stack.enter_context(nc.psum_tensor("ps", [P, 8, 512], F32))

        count_cst_in = sem("count_cst_in")
        cst_in = sem("cst_in")
        tok_in = sem("tok_in")
        scale_in = sem("scale_in")
        down_scale_in = sem("down_scale_in")
        expert_in = [sem(f"expert_in{e}") for e in range(EXPERTS)]
        slice_in = sem("slice_in")
        slice_used = sem("slice_used")
        gate_up_short = sem("gate_up_short")
        down_short = sem("down_short")
        x_in = [sem(f"x_in{q}") for q in range(EARLY + 1)]
        out_done = [sem(f"out_done{t}") for t in range(CT)]
        out_free = sem("out_free")
        again_in = sem("again_in")
        again_used = sem("again_used")
        dve_step = sem("dve_step")
        pool_step = sem("pool_step")
        rest_step = sem("rest_step")
        member_ready = sem("member_ready")
        counts_ready = sem("counts_ready")
        hot_ready = sem("hot_ready")
        tile_hot_ready = sem("tile_hot_ready")
        tile_tok_ready = sem("tile_tok_ready")
        order_psum = sem("order_psum")
        order_ready = sem("order_ready")
        units_ready = sem("units_ready")
        half_ready = sem("half_ready")
        expert_high = sem("expert_high")
        expert_low = sem("expert_low")
        count_ready = sem("count_ready")
        count_psum = sem("count_psum")
        general_ready = sem("general_ready")
        u_bn = sem("u_bn")
        bn_seen = sem("bn_seen")
        u_stats = sem("u_stats")
        u_rstd = sem("u_rstd")
        u_norm = sem("u_norm")
        u_xt = sem("u_xt")
        u_xt_high = sem("u_xt_high")
        u_xt_low = sem("u_xt_low")
        u_up = sem("u_up")
        u_silu = sem("u_silu")
        u_hid = sem("u_hid")
        u_ht = sem("u_ht")
        u_ht_high = sem("u_ht_high")
        u_ht_low = sem("u_ht_low")
        u_down = sem("u_down")
        x_now = sem("x_now")
        c_bn = sem("c_bn")
        c_stats = sem("c_stats")
        c_rstd = sem("c_rstd")
        t_norm = sem("t_norm")
        t_xt = sem("t_xt")
        t_high = sem("t_high")
        t_low = sem("t_low")
        s_gate = sem("s_gate")
        s_up = sem("s_up")
        s_silu = sem("s_silu")
        s_hid = sem("s_hid")
        s_high = sem("s_high")
        s_low = sem("s_low")
        s_rest = sem("s_rest")
        s_down = sem("s_down")
        acc_full = sem("acc_full")
        acc_free = sem("acc_free")
        out_ready = sem("out_ready")

        ident = cst[:, C_IDENT:C_IDENT + P]
        slot_hot = xt[:, 0, :, :].rearrange("p k t -> p (k t)").rearrange("p (c s) -> p c s", s=P)
        left_out = xt[:, 2:4, :, :].rearrange("p a k t -> p (a k t)").bitcast(F32)[:, 0:SLICE_W]
        rest_gu = [stage[:, 1, j * D:(j + 1) * D].bitcast(BF16) for j in range(2)]

        expert_raw = [stage[:, 0, :], stage[:, 1, :], outb[:, :, :].rearrange("p t d -> p (t d)"),
                      w1[:, SLICES * 2 * D - 2 * KD * D:].bitcast(F32)]

        def rest_d(i):
            return ew[:, (i % 2) * D:(i % 2 + 1) * D]

        def ew_half(e, part):
            return ew[:, (e * 2 + part) * KD * D:(e * 2 + part + 1) * KD * D]

        def ew_at(e, part, k):
            return ew[:, bass.ds(e * (2 * KD * D) + (part * KD + k) * D, D)]

        def xs_at(q):
            return xs[:, bass.ds(q * D, D)]

        def cols(a, n=P):
            return slice(a * n, (a + 1) * n)

        block = stack.enter_context(nc.Block())

        @block.sync
        def _(sp):
            sp.dma_start(tok_sb[:, :], tok).then_inc(tok_in, 16)
            sp.dma_start(cst[:, 0:2 * P], consts[:, 0:2 * P]).then_inc(count_cst_in, 16)
            sp.dma_start(cst[:, 2 * P:C_ALL], consts[:, 2 * P:C_ALL]).then_inc(cst_in, 16)
            sp.dma_start(gu_s[:, :], scales).then_inc(scale_in, 16)
            for e in range(EXPERTS):
                if e >= 2:
                    sp.wait_ge(x_in[0 if e == 2 else 2], 16)
                sp.dma_start(expert_raw[e], ctx_t[e]).then_inc(expert_in[e], 16)
            sp.dma_start(ds_row[:, :], down_s).then_inc(down_scale_in, 16)
            sp.wait_ge(expert_low, 2 * 2)
            for s in range(SLICES):
                if s >= 1:
                    sp.wait_ge(slice_in, 16 * s)
                if s >= 2:
                    sp.wait_ge(slice_used, s - 1)
                sp.dma_start(stage[:, s % 2, 0:SLICE_W], ffn_w[s]).then_inc(slice_in, 16)
            sp.wait_ge(general_ready, 1)
            general = sp.value_load(general_i[0:1, 0:1])
            with sp.If(general):
                with sp.Fori(0, CHUNKS) as c:
                    for s in range(SLICES):
                        sp.wait_ge(again_used, c * SLICES + s + 1)
                        sp.dma_start(stage[:, 0, 0:SLICE_W], ffn_w[s]).then_inc(again_in, 16)
            with sp.Else():
                pass

        def chunk_rstd(pool, c):
            pool.wait_ge(c_stats, c + 1)
            pool.tensor_scalar(rstd[:, 0, :], mv[:, :, 1:2].rearrange("p t a -> p (t a)"), EPS, None,
                               ALU.add).then_inc(pool_step, 1)
            pool.wait_ge(pool_step, 2 * UNITS + 2 * c + 1)
            pool.tensor_tensor(rstd[:, 1, :], rstd[:, 0, :], half_neg[:, :], ALU.pow).then_inc(pool_step, 1)
            pool.wait_ge(pool_step, 2 * UNITS + 2 * c + 2)
            pool.tensor_scalar(rstd[:, 2, :], rstd[:, 1, :], XSCALE, None, ALU.mult).then_inc(c_rstd, 1)

        @block.gpsimd
        def _(pool):
            pool.sem_inc(again_used, 1)
            pool.sem_inc(out_free, CT)
            pool.memset(half_neg[:, :], -0.5).then_inc(half_ready, 1)
            pool.memset(eps[:, :], EPS).then_inc(half_ready, 1)

            def unit_rstd(u):
                pool.wait_ge(u_stats, u + 1)
                pool.tensor_tensor(rstd_u[:, 0:1], mv_u[:, 1:2], eps[:, :], ALU.add).then_inc(pool_step, 1)
                pool.wait_ge(pool_step, 2 * u + 1)
                pool.tensor_tensor(rstd_u[:, 1:2], rstd_u[:, 0:1], half_neg[:, 0:1], ALU.pow).then_inc(pool_step, 1)
                pool.wait_ge(pool_step, 2 * u + 2)
                pool.tensor_tensor(rstd_u[:, 2:3], rstd_u[:, 1:2], mask[:, bass.ds(u, 1)],
                                   ALU.mult).then_inc(u_rstd, 1)

            def remainder(s):
                raw = stage[:, bass.ds(s % 2, 1), 0:SLICE_W].rearrange("p a w -> p (a w)")
                pool.wait_ge(gate_up_short, s + 1)
                if not isinstance(s, int) or s >= 1:
                    pool.wait_ge(count_ready, s)
                pool.tensor_tensor(left_out[:, 0:2 * D], raw[:, 0:2 * D], w1[:, bass.ds(s * (2 * D), 2 * D)],
                                   ALU.subtract)
                pool.wait_ge(down_short, s + 1)
                pool.tensor_tensor(left_out[:, 2 * D:3 * D], raw[:, 2 * D:3 * D],
                                   wd[:, bass.ds(s * D, D)].bitcast(F32), ALU.subtract).then_inc(slice_used, 1)

            pool.wait_ge(tile_hot_ready, 1)
            pool.tensor_tensor(tile_tok[:, :, :], tile_hot[:, :, :],
                               cst[:, C_TOKEN:C_TOKEN + TILES].unsqueeze(2).broadcast_to([P, TILES, TILES]),
                               ALU.mult).then_inc(tile_tok_ready, 1)
            pool.wait_ge(order_ready, 1)
            for q in range(TILES):
                pool.indirect_dma_start(
                    xs[:, q * D:(q + 1) * D], None, x,
                    bass.IndirectOffsetOnAxis(ap=order[:, q:q + 1], axis=0)).then_inc(x_in[min(q, EARLY)], 16)
                if q in FACTOR_AFTER:
                    pool.wait_ge(units_ready, 1)
                    if q == FACTOR_AFTER[-1]:
                        remainder(0)
                    unit_rstd(FACTOR_AFTER.index(q))

            with pool.Fori(1, SLICES) as s:
                remainder(s)
                unit_rstd(s + EARLY_UNITS - 1)
            with pool.Fori(EARLY_UNITS - 1 + SLICES, UNITS) as u:
                unit_rstd(u)
            for c in range(CHUNKS):
                if c == 0:
                    chunk_rstd(pool, 0)
                if c + 1 < CHUNKS:
                    chunk_rstd(pool, c + 1)
                for t in range(CT):
                    q = c * CT + t
                    pool.wait_ge(out_ready, q + 1)
                    pool.indirect_dma_start(
                        out, bass.IndirectOffsetOnAxis(ap=order[:, q:q + 1], axis=0),
                        outb[:, t, :], None).then_inc(out_done[t], 16)
                for t in range(CT):
                    pool.wait_ge(out_done[t], 16 * c + 16)
                    pool.sem_inc(out_free, 1)

        @block.scalar
        def _(act):
            act.wait_ge(half_ready, 2)
            act.activation(warm[:, :], half_neg[:, 0:1], ACT.Silu)

            def high(e):
                act.wait_ge(expert_in[e], 16)
                act.activation(ew_half(e, 0), expert_raw[e], ACT.Copy).then_inc(expert_high, 1)

            def xt_high(u):
                act.wait_ge(u_xt, u + 1)
                act.activation(halves[:, 0, 0, :], ps[:, B_UX, :], ACT.Copy).then_inc(u_xt_high, 1)

            def silu(u):
                act.wait_ge(u_up, u + 1)
                act.activation(gate[:, :], ps[:, B_G, :], ACT.Silu).then_inc(u_silu, 1)

            def ht_high(u):
                act.wait_ge(u_ht, u + 1)
                act.activation(halves[:, 1, 0, :], ps[:, B_HT, :], ACT.Copy).then_inc(u_ht_high, 1)

            def shorten_gate_up(s):
                act.wait_ge(slice_in, 16 * s + 16)
                act.activation(w1[:, bass.ds(s * (2 * D), 2 * D)],
                               stage[:, bass.ds(s % 2, 1), 0:2 * D].rearrange("p a w -> p (a w)"),
                               ACT.Copy).then_inc(gate_up_short, 1)

            def shorten_down(s):
                act.activation(wd[:, bass.ds(s * D, D)],
                               stage[:, bass.ds(s % 2, 1), 2 * D:3 * D].rearrange("p a w -> p (a w)"),
                               ACT.Copy).then_inc(down_short, 1)

            def sum_left_out(s):
                act.wait_ge(slice_used, s + 1)
                act.activation(left_out, left_out, ACT.Abs,
                               accum_out=inexact[:, bass.ds(s, 1)]).then_inc(count_ready, 1)

            high(0)
            high(1)
            xt_high(0)
            high(2)
            silu(0)
            xt_high(1)
            ht_high(0)
            high(3)
            silu(1)
            xt_high(2)
            shorten_gate_up(0)
            ht_high(1)
            shorten_down(0)
            silu(2)
            xt_high(3)
            shorten_gate_up(1)
            with act.Fori(3, SLICES + 1) as u:
                ht_high(u - 1)
                sum_left_out(u - 3)
                shorten_down(u - 2)
                silu(u)
                xt_high(u + 1)
                shorten_gate_up(u - 1)
            ht_high(SLICES)
            sum_left_out(SLICES - 2)
            shorten_down(SLICES - 1)
            silu(SLICES + 1)
            xt_high(SLICES + 2)
            ht_high(SLICES + 1)
            sum_left_out(SLICES - 1)
            silu(SLICES + 2)
            xt_high(SLICES + 3)
            with act.Fori(SLICES + 3, UNITS - 1) as u:
                ht_high(u - 1)
                silu(u)
                xt_high(u + 1)

            def tile_high(t, slot, tt, bank):
                act.wait_ge(t_xt, t + 1)
                act.activation(xt[:, bass.ds(2 * slot, 1), :, cols(tt)].rearrange("p a k t -> p (a k) t"),
                               ps[:, bank, :].rearrange("p (k t) -> p k t", k=KD),
                               ACT.Copy).then_inc(t_high, 1)

            ht_high(UNITS - 2)
            silu(UNITS - 1)
            ht_high(UNITS - 1)
            for t in range(CT):
                tile_high(t, 0, t, FIRST_XT[t])

            def last_slice():
                i, n = SLICES - 1, CHUNKS * SLICES - 1
                for h in range(2):
                    half = cols(h, HALF)
                    act.wait_ge(s_gate, n + 1 + h)
                    act.wait_ge(s_hid, n)
                    act.activation(gate[:, half], ps[:, HALF_BANKS[h][0], half], ACT.Silu,
                                   scale=gate_sx[:, i:i + 1]).then_inc(s_silu, 1)
                    act.wait_ge(s_hid, n + 1 + h)
                    act.activation(halves[:, i % 2, 0, half], hid[:, half], ACT.Copy).then_inc(s_high, 1)

            def chunk(c, last):
                for i in range(SLICES - 1 if last else SLICES):
                    n = c * SLICES + i
                    act.wait_ge(s_gate, n + 1)
                    if i >= 1:
                        act.wait_ge(s_hid, n)
                    act.activation(gate[:, :], ps[:, B_G, :], ACT.Silu, scale=gate_sx[:, i:i + 1]).then_inc(s_silu, 1)
                    act.wait_ge(s_hid, n + 1)
                    act.activation(halves[:, i % 2, 0, :], hid[:, :], ACT.Copy).then_inc(s_high, 1)
                    for t in range(CT):
                        if not last and TURN_AT[t] == i:
                            tile_high(c * CT + CT + t, (c + 1) % 2, t, B_XT + t % 2)

            with act.Fori(0, CHUNKS - 1) as c:
                chunk(c, False)
            chunk(CHUNKS - 1, True)
            last_slice()

        @block.vector
        def _(dve):
            steps = [0]

            def step(ins):
                steps[0] += 1
                ins.then_inc(dve_step, 1)
                dve.wait_ge(dve_step, steps[0])

            dve.memset(zeros[:, :], 0.0)
            dve.memset(base[:, 3:4], float(TOKENS))
            dve.memset(near[0:1, :, :], 0)
            dve.wait_ge(tok_in, 16)
            for e in range(1, EXPERTS):
                last = dve.tensor_scalar(ge[:, e - 1, :], tok_sb[:, :], float(e * PER_EXPERT), None, ALU.is_ge)
            step(last)
            dve.tensor_scalar(member[:, 0, :], ge[:, 0, :], -1.0, 1.0, ALU.mult, ALU.add)
            dve.tensor_tensor(member[:, 1:3, :], ge[:, 0:2, :], ge[:, 1:3, :], ALU.subtract)
            dve.tensor_copy(member[:, 3, :], ge[:, 2, :]).then_inc(member_ready, 1)
            dve.wait_ge(counts_ready, 1)
            totals = ps[:, B_ACC + 2, 0:EXPERTS * TILES]
            earlier = ps[:, B_ACC + 2, P:P + EXPERTS * TILES]
            step(dve.tensor_tensor_scan(upto[:, :], totals, zeros[:, :], 0.0, ALU.add, ALU.add))
            step(dve.tensor_tensor(before[:, :], upto[:, :], totals, ALU.subtract))
            step(dve.tensor_tensor(rank[:, :, :].rearrange("p e c -> p (e c)"), earlier, before[:, :], ALU.add))
            step(dve.tensor_tensor(rank[:, :, :], rank[:, :, :], member[:, :, :], ALU.mult))
            with nc.allow_low_precision(reason="whole numbers below TOKENS"):
                step(dve.tensor_reduce(pos_i[:, 0, :], rank[:, :, :].rearrange("p e c -> p c e"), AX, ALU.add))
            dve.tensor_scalar(pos_i[:, 2, :], pos_i[:, 0, :], 7, None, ALU.logical_shift_right)
            step(dve.tensor_scalar(pos_i[:, 1, :], pos_i[:, 0, :], P - 1, None, ALU.bitwise_and))
            dve.wait_ge(cst_in, 16)
            unit_row = cst[:, C_UNIT:C_UNIT + UNITS]
            step(dve.tensor_tensor(tile_hot[:, :, :], pos_i[:, 2, :].unsqueeze(2).broadcast_to([P, TILES, TILES]),
                                   cst[:, C_TILE:C_TILE + TILES].unsqueeze(1).broadcast_to([P, TILES, TILES]),
                                   ALU.is_equal))
            dve.sem_inc(tile_hot_ready, 1)
            dve.tensor_tensor(slot_hot, pos_i[:, 1, :].unsqueeze(2).broadcast_to([P, TILES, P]),
                              cst[:, C_SLOT:C_SLOT + P].unsqueeze(1).broadcast_to([P, TILES, P]),
                              ALU.is_equal).then_inc(hot_ready, 1)
            dve.tensor_copy(base[:, 0:3], before[:, TILES::TILES])
            step(dve.tensor_copy(first_i[:, 0, :], before[:, TILES::TILES]))
            step(dve.tensor_scalar(first_i[:, 1, :], first_i[:, 0, :], 7, None, ALU.logical_shift_right))
            step(dve.tensor_tensor(first_unit[:, :], first_i[:, 1, :], cst[:, C_TILE + 1:C_TILE + EXPERTS], ALU.add))
            step(dve.tensor_tensor(u_ge[:, :, :], unit_row.unsqueeze(1).broadcast_to([P, 3, UNITS]),
                                   first_unit[:, :].unsqueeze(2).broadcast_to([P, 3, UNITS]), ALU.is_ge))
            dve.wait_ge(order_psum, 1)
            dve.tensor_copy(order[:, :], ps[:, B_ACC + 3, 0:TILES]).then_inc(order_ready, 1)
            step(dve.tensor_reduce(u_expert[:, :], u_ge[:, :, :].rearrange("p e u -> p u e"), AX, ALU.add))
            step(dve.tensor_tensor(u_tile[:, 0, :], unit_row, u_expert[:, :], ALU.subtract))
            dve.tensor_scalar(u_tile[:, 1, :], u_tile[:, 0, :], float(TILES - 1), None, ALU.min)
            step(dve.tensor_scalar(u_row[:, :], u_tile[:, 0, :], float(P), cst[:, C_PART:C_PART + 1],
                                   ALU.mult, ALU.add))
            step(dve.tensor_tensor(row_ge[:, :, :], u_row[:, :].unsqueeze(1).broadcast_to([P, EXPERTS, UNITS]),
                                   base[:, :].unsqueeze(2).broadcast_to([P, EXPERTS, UNITS]), ALU.is_ge))
            step(dve.tensor_reduce(row_expert[:, :], row_ge[:, :, :].rearrange("p e u -> p u e"), AX, ALU.add))
            dve.tensor_tensor(mask[:, :], row_expert[:, :], u_expert[:, :], ALU.is_equal)
            dve.tensor_copy(near[0:1, 1:UNITS + 1, 0], u_tile[0:1, 1, :])
            dve.tensor_copy(near[0:1, 0:UNITS - 2, 1], u_tile[0:1, 1, 2:UNITS])
            dve.tensor_copy(near[0:1, 0:UNITS - 3, 2], u_tile[0:1, 1, 3:UNITS])
            dve.tensor_copy(unit_expert[0:1, :], u_expert[0:1, :]).then_inc(units_ready, 1)
            dve.wait_ge(units_ready, 1)

            def expert_rest(e, part):
                half = slice(part * KD * D // 2, (part + 1) * KD * D // 2)
                dve.wait_ge(expert_high, e + 1)
                dve.tensor_tensor(ew_half(e, 1)[:, half], expert_raw[e][:, half],
                                  ew_half(e, 0)[:, half].bitcast(F32), ALU.subtract).then_inc(expert_low, 1)

            def tiles_near(u):
                _, q = nc.values_load_multi_w_load_instructions(
                    near[0:1, bass.ds(u, 1), 0:3].rearrange("p a q -> p (a q)"),
                    engines=(mybir.EngineType.DVE,), min_val=0, max_val=TILES - 1)
                return q

            def stats(u, q):
                if isinstance(u, int) and u < EARLY:
                    dve.wait_ge(x_in[u], 16)
                else:
                    dve.wait_ge(x_in[EARLY], 16 * (TILES - EARLY))
                if not isinstance(u, int) or u >= 1:
                    dve.wait_ge(u_norm, u)
                dve.bn_stats(bn6_u[:, :], xs_at(q)).then_inc(u_bn, 1)
                dve.wait_ge(u_bn, u + 1)
                dve.sem_inc(bn_seen, 1)
                dve.bn_aggr(mv_u[:, :], bn6_u[:, :]).then_inc(u_stats, 1)

            def stats_first(u):
                q = 0 if u == 0 else dve.value_load(near[0:1, u + 1, 0:1], min_val=0, max_val=u)
                stats(u, q)
                return q

            def norm(u, q):
                dve.wait_ge(u_rstd, u + 1)
                dve.tensor_scalar(xn[:, 0, :], xs_at(q), mv_u[:, 0:1], rstd_u[:, 2:3],
                                  ALU.subtract, ALU.mult).then_inc(u_norm, 1)

            def xt_low(u):
                dve.wait_ge(u_xt_high, u + 1)
                dve.tensor_tensor(halves[:, 0, 1, :], ps[:, B_UX, :], halves[:, 0, 0, :].bitcast(F32),
                                  ALU.subtract).then_inc(u_xt_low, 1)

            def hidden(u):
                dve.wait_ge(u_silu, u + 1)
                dve.tensor_tensor(hid[:, :], ps[:, B_G, :], gate[:, :], ALU.mult).then_inc(u_hid, 1)

            def ht_low(u):
                dve.wait_ge(u_ht_high, u + 1)
                dve.tensor_tensor(halves[:, 1, 1, :], ps[:, B_HT, :], halves[:, 1, 0, :].bitcast(F32),
                                  ALU.subtract).then_inc(u_ht_low, 1)

            def add(u, q):
                dve.wait_ge(u_down, u + 1)
                dve.tensor_tensor(xs_at(q), ps[:, B_U, :], xs_at(q), ALU.add).then_inc(x_now, 1)

            def unit(u, norms, statistics):
                hidden(u)
                xt_low(u + 1)
                q = tiles_near(u)
                add(u - 1, q[0])
                if norms:
                    dve.wait_ge(x_now, u + 1)
                    norm(u + 2, q[1])
                ht_low(u)
                if statistics:
                    stats(u + 3, q[2])

            def chunk_stats(c, t):
                dve.bn_stats(bn6[:, t, :], xs_at(c * CT + t)).then_inc(c_bn, 1)

            def chunk_aggr(t):
                ins = dve.bn_aggr(mv[:, t, :], bn6[:, t, :])
                if t == CT - 1:
                    ins.then_inc(c_stats, 1)

            def tile_norm(c, t, dst):
                n = c * CT + t
                dve.wait_ge(c_rstd, c + 1)
                dve.tensor_scalar(dst, xs_at(n), mv[:, t, 0:1], rstd[:, 2, t:t + 1],
                                  ALU.subtract, ALU.mult).then_inc(t_norm, 1)

            def tile_low(c, slot, t, bank):
                n = c * CT + t
                dve.wait_ge(t_high, n + 1)
                dve.tensor_tensor(xt[:, bass.ds(2 * slot + 1, 1), :, cols(t)].rearrange("p a k t -> p (a k) t"),
                                  ps[:, bank, :].rearrange("p (k t) -> p k t", k=KD),
                                  xt[:, bass.ds(2 * slot, 1), :, cols(t)].rearrange("p a k t -> p (a k) t"),
                                  ALU.subtract).then_inc(t_low, 1)

            expert_rest(0, 0)
            q = stats_first(0)
            expert_rest(0, 1)
            norm(0, q)
            q = stats_first(1)
            xt_low(0)
            expert_rest(1, 0)
            dve.wait_ge(u_xt, 1)
            norm(1, q)
            expert_rest(1, 1)
            dve.wait_ge(scale_in, 16)
            dve.tensor_scalar(gate_sx[:, :], gu_s[:, :], 1.0 / XSCALE, None, ALU.mult).then_inc(x_now, 1)
            hidden(0)
            xt_low(1)
            q = stats_first(2)
            ht_low(0)
            norm(2, q)
            expert_rest(2, 0)
            stats_first(3)
            unit(1, True, True)
            expert_rest(2, 1)
            expert_rest(3, 0)
            unit(2, True, True)
            expert_rest(3, 1)
            dve.wait_ge(down_scale_in, 16)
            with dve.Fori(3, UNITS - 3) as u:
                unit(u, True, True)
            unit(UNITS - 3, True, False)
            for t in range(CT - 1):
                chunk_stats(0, t)
            q = dve.value_load(near[0:1, UNITS - 2, 0:1], min_val=0, max_val=TILES - 1)
            hidden(UNITS - 2)
            xt_low(UNITS - 1)
            chunk_stats(0, CT - 1)
            dve.wait_ge(c_bn, CT)
            for t in range(CT):
                chunk_aggr(t)
            add(UNITS - 3, q)
            ht_low(UNITS - 2)
            dve.wait_ge(count_ready, SLICES)
            dve.tensor_reduce(inexact_p[:, 0:1], inexact[:, :], AX, ALU.add).then_inc(count_ready, 1)
            dve.wait_ge(count_ready, SLICES + 1)
            dve.tensor_scalar(inexact_p[:, 1:2], inexact_p[:, 0:1], 0.0, None, ALU.not_equal).then_inc(count_ready, 1)
            q_before = dve.value_load(near[0:1, UNITS - 1, 0:1], min_val=0, max_val=TILES - 1)
            tile_norm(0, 0, outb[:, 0, :])
            hidden(UNITS - 1)
            for t in range(1, CT):
                tile_norm(0, t, outb[:, t, :])
            dve.wait_ge(x_now, UNITS - 1)
            add(UNITS - 2, q_before)
            ht_low(UNITS - 1)
            dve.wait_ge(count_psum, 1)
            dve.tensor_copy(general_i[0:1, 0:1], ps[0:1, B_ACC + 3, 0:1]).then_inc(general_ready, 1)
            for t in range(CT):
                tile_low(0, 0, t, FIRST_XT[t])
            q_last = dve.value_load(near[0:1, UNITS, 0:1], min_val=0, max_val=TILES - 1)
            dve.wait_ge(x_now, UNITS)
            add(UNITS - 1, q_last)
            dve.wait_ge(x_now, UNITS + 1)
            dve.sem_inc(acc_free, 1)
            dve.wait_ge(general_ready, 1)
            general = dve.value_load(general_i[0:1, 0:1])

            def remainders(c, i):
                n = c * SLICES + i
                raw_gu, raw_d = stage[:, 0, 0:2 * D], stage[:, 0, 2 * D:3 * D]
                dve.wait_ge(again_in, 16 * n + 16)
                if i >= 2:
                    dve.wait_ge(s_down, c * (SLICES - 1) + i - 1)
                if i >= 1:
                    dve.wait_ge(s_up, n)
                dve.tensor_tensor(raw_gu, raw_gu, w1[:, i * 2 * D:(i + 1) * 2 * D],
                                  ALU.subtract).then_inc(rest_step, 1)
                dve.wait_ge(rest_step, 2 * n + 1)
                dve.tensor_copy(rest_gu[0], raw_gu).then_inc(rest_step, 1)
                dve.wait_ge(rest_step, 2 * n + 2)
                dve.tensor_tensor(rest_gu[1], raw_gu, rest_gu[0], ALU.subtract)
                dve.tensor_tensor(rest_d(i), raw_d, wd[:, i * D:(i + 1) * D].bitcast(F32),
                                  ALU.subtract).then_inc(s_rest, 1)
                dve.wait_ge(s_rest, n + 1)
                dve.sem_inc(again_used, 1)

            def last_slice():
                i, n = SLICES - 1, CHUNKS * SLICES - 1
                for h in range(2):
                    half = cols(h, HALF)
                    dve.wait_ge(s_low, n)
                    dve.wait_ge(s_up, n + 1 + h)
                    dve.wait_ge(s_silu, n + 1 + h)
                    dve.scalar_tensor_tensor(hid[:, half], ps[:, HALF_BANKS[h][1], half],
                                             gate_sx[:, SLICES + i:SLICES + i + 1],
                                             gate[:, half], ALU.mult, ALU.mult).then_inc(s_hid, 1)
                    dve.wait_ge(s_high, n + 1 + h)
                    dve.tensor_tensor(halves[:, i % 2, 1, half], hid[:, half],
                                      halves[:, i % 2, 0, half].bitcast(F32), ALU.subtract).then_inc(s_low, 1)

            def chunk(c, last, rest):
                for i in range(SLICES):
                    n = c * SLICES + i
                    if rest:
                        remainders(c, i)
                    if last and i == SLICES - 1:
                        last_slice()
                        break
                    if not last and i == 1:
                        dve.wait_ge(c_bn, CT * c + 2 * CT)
                    if i >= 1:
                        dve.wait_ge(s_low, n)
                    dve.wait_ge(s_up, n + 1)
                    dve.wait_ge(s_silu, n + 1)
                    dve.scalar_tensor_tensor(hid[:, :], ps[:, B_U, :], gate_sx[:, SLICES + i:SLICES + i + 1],
                                             gate[:, :], ALU.mult, ALU.mult).then_inc(s_hid, 1)
                    if not last and i == 1:
                        for t in range(CT):
                            chunk_aggr(t)
                    dve.wait_ge(s_high, n + 1)
                    dve.tensor_tensor(halves[:, i % 2, 1, :], hid[:, :], halves[:, i % 2, 0, :].bitcast(F32),
                                      ALU.subtract).then_inc(s_low, 1)
                    if not last and i == 0:
                        for t in range(CT):
                            chunk_stats(c + 1, t)
                    for t in range(CT):
                        if not last and TURN_AT[t] == i:
                            tile_low(c + 1, (c + 1) % 2, t, B_XT + t % 2)
                    if not last and i in NORM_AT:
                        t = NORM_AT.index(i)
                        if t >= 2:
                            dve.wait_ge(t_xt, c * CT + CT + t - 1)
                        tile_norm(c + 1, t, xn[:, t % 2, :])

                def scale_out(t):
                    dve.wait_ge(acc_full, c * CT + t + 1)
                    dve.wait_ge(out_free, c * CT + t + 1)
                    dve.tensor_tensor(outb[:, t, :], ps[:, B_ACC + t, :], ds_row[:, :],
                                      ALU.mult).then_inc(acc_free, 1)

                def sum_out(t):
                    dve.wait_ge(acc_free, c * CT + t + 2)
                    dve.tensor_tensor(outb[:, t, :], outb[:, t, :], xs_at(c * CT + t),
                                      ALU.add).then_inc(out_ready, 1)

                for t in range(CT):
                    scale_out(t)
                    if t >= 1:
                        sum_out(t - 1)
                sum_out(CT - 1)

            def dense(rest):
                with dve.Fori(0, CHUNKS - 1) as c:
                    chunk(c, False, rest)
                chunk(CHUNKS - 1, True, rest)

            with dve.If(general):
                dense(True)
            with dve.Else():
                dense(False)

        @block.tensor
        def _(pe):
            pe.wait_ge(count_cst_in, 16)
            pe.wait_ge(member_ready, 1)
            members = member[:, :, :].rearrange("p e c -> p (e c)")
            n_cols = EXPERTS * TILES
            pe.matmul(ps[:, B_ACC + 2, 0:n_cols], cst[:, C_ONES:C_ONES + P], members, start=True, stop=True)
            pe.matmul(ps[:, B_ACC + 2, P:P + n_cols], cst[:, C_BEFORE:C_BEFORE + P], members,
                      start=True, stop=True).then_inc(counts_ready, 1)
            pe.wait_ge(cst_in, 16)
            pe.wait_ge(tile_tok_ready, 1)
            pe.wait_ge(hot_ready, 1)
            for c in range(TILES):
                mm = pe.matmul(ps[:, B_ACC + 3, 0:TILES], slot_hot[:, c, :], tile_tok[:, c, :],
                               start=(c == 0), stop=(c == TILES - 1))
            mm.then_inc(order_psum, 1)
            for _ in range(WARM_UP):
                pe.matmul(ps[:, B_ACC, 0:P], ident, cst[:, C_SLOT:C_SLOT + P], start=True, stop=True)
            pe.wait_ge(units_ready, 1)

            def expert_of(u):
                return pe.value_load(unit_expert[0:1, bass.ds(u, 1)], min_val=0, max_val=EXPERTS - 1)

            def split_product(dst, slot, e, high_ready, low_ready, u):
                passes = [(k, 0, b) for k in range(KD) for b in range(2)] + [(k, 1, 0) for k in range(KD)]
                for n, (k, a, b) in enumerate(passes):
                    if n == 0:
                        pe.wait_ge(high_ready, u + 1)
                    elif n == 2 * KD:
                        pe.wait_ge(low_ready, u + 1)
                    mm = pe.matmul(dst, halves[:, slot, a, cols(k)], ew_at(e, b, k),
                                   start=(n == 0), stop=(n == len(passes) - 1))
                return mm

            def turn(bank, src):
                for k in range(KD):
                    mm = pe.transpose(ps[:, bank, cols(k)], src[:, cols(k)], ident)
                return mm

            def turn_x(u):
                pe.wait_ge(u_norm, u + 1)
                turn(B_UX, xn[:, 0, :]).then_inc(u_xt, 1)

            def up(u, e):
                pe.wait_ge(expert_low, 2 * e + 2)
                split_product(ps[:, B_G, :], 0, e, u_xt_high, u_xt_low, u).then_inc(u_up, 1)

            def turn_h(u):
                pe.wait_ge(u_hid, u + 1)
                turn(B_HT, hid).then_inc(u_ht, 1)

            def down(u, e):
                pe.wait_ge(x_now, u + 1)
                split_product(ps[:, B_U, :], 1, e, u_ht_high, u_ht_low, u).then_inc(u_down, 1)

            second = expert_of(1)
            turn_x(0)
            up(0, 0)
            turn_x(1)
            turn_h(0)
            up(1, second)
            with pe.Fori(1, UNITS - 1) as u:
                done = expert_of(u - 1)
                turn_x(u + 1)
                down(u - 1, done)
                coming = expert_of(u + 1)
                turn_h(u)
                up(u + 1, coming)

            def turn_tile(t, src, bank):
                pe.wait_ge(t_norm, t + 1)
                turn(bank, src).then_inc(t_xt, 1)

            before_last, last_one = expert_of(UNITS - 2), expert_of(UNITS - 1)
            down(UNITS - 2, before_last)
            turn_h(UNITS - 1)
            pe.wait_ge(count_ready, SLICES + 2)
            pe.matmul(ps[:, B_ACC + 3, 0:1], cst[:, C_ONES:C_ONES + P], inexact_p[:, 1:2],
                      start=True, stop=True).then_inc(count_psum, 1)
            for t in range(CT):
                turn_tile(t, outb[:, t, :], FIRST_XT[t])
            down(UNITS - 1, last_one)
            pe.wait_ge(general_ready, 1)
            general = pe.value_load(general_i[0:1, 0:1])

            def gate_or_up(bank, i, which, slot, rest, tokens=slice(0, CHUNK)):
                at = (i * 2 + which) * D
                parts = []
                for k in range(KD):
                    parts += [(w1[:, at + k * P:at + (k + 1) * P], 0, k), (w1[:, at + k * P:at + (k + 1) * P], 1, k)]
                    if rest:
                        r = [rest_gu[j][:, which * D + k * P:which * D + (k + 1) * P] for j in range(2)]
                        parts += [(r[0], 0, k), (r[0], 1, k), (r[1], 0, k)]
                for n, (w, part, k) in enumerate(parts):
                    mm = pe.matmul(ps[:, bank, tokens], w,
                                   xt[:, bass.ds(2 * slot + part, 1), k, tokens].rearrange("p a t -> p (a t)"),
                                   start=(n == 0), stop=(n == len(parts) - 1))
                return mm

            def slice_down(c, i, rest, tiles=range(CT)):
                n = c * SLICES + i
                in_halves = len(tiles) < CT and i == SLICES - 1
                pe.wait_ge(s_low, n + 1 + (tiles[0] // len(tiles) if in_halves else 0))
                if i == 0:
                    pe.wait_ge(acc_free, c * CT + 1)
                for t in tiles:
                    rhs = wd[:, i * D:(i + 1) * D]
                    pairs = [(0, rhs), (1, rhs)]
                    if rest:
                        pairs += [(0, rest_d(i)), (1, rest_d(i))]
                    for m, (part, r) in enumerate(pairs):
                        mm = pe.matmul(ps[:, B_ACC + t, :], halves[:, i % 2, part, cols(t)], r,
                                       start=(i == 0 and m == 0), stop=(i == SLICES - 1 and m == len(pairs) - 1))
                    if i == SLICES - 1:
                        mm.then_inc(acc_full, 1)
                if rest and i < SLICES - 1 and tiles[-1] == CT - 1:
                    mm.then_inc(s_down, 1)

            def last_slice(rest):
                c, i = CHUNKS - 1, SLICES - 1
                n = c * SLICES + i
                pe.wait_ge(s_silu, n)
                if rest:
                    pe.wait_ge(s_rest, n + 1)
                for h in range(2):
                    gate_or_up(HALF_BANKS[h][0], i, 0, c % 2, rest, cols(h, HALF)).then_inc(s_gate, 1)
                    pe.wait_ge(s_hid, n)
                    gate_or_up(HALF_BANKS[h][1], i, 1, c % 2, rest, cols(h, HALF)).then_inc(s_up, 1)
                for h in range(2):
                    tiles = range(h * CT // 2, (h + 1) * CT // 2)
                    slice_down(c, i - 1, rest, tiles)
                    slice_down(c, i, rest, tiles)

            def chunk(c, last, rest):
                slot = c % 2
                for i in range(SLICES - 1 if last else SLICES):
                    n = c * SLICES + i
                    if i == 0:
                        pe.wait_ge(t_low, c * CT + CT)
                    else:
                        pe.wait_ge(s_silu, n)
                    if rest:
                        pe.wait_ge(s_rest, n + 1)
                    gate_or_up(B_G, i, 0, slot, rest).then_inc(s_gate, 1)
                    if i >= 1:
                        pe.wait_ge(s_hid, n)
                    elif not isinstance(c, int) or c == 0:
                        pe.wait_ge(x_now, UNITS + 1)
                    gate_or_up(B_U, i, 1, slot, rest).then_inc(s_up, 1)
                    for t in range(CT):
                        if not last and TURN_AT[t] == i:
                            pe.wait_ge(t_low, c * CT + CT + t - 1)
                            turn_tile(c * CT + CT + t, xn[:, t % 2, :], B_XT + t % 2)
                    if i >= 1:
                        slice_down(c, i - 1, rest)
                if last:
                    last_slice(rest)
                else:
                    slice_down(c, SLICES - 1, rest)

            def dense(rest):
                with pe.Fori(0, CHUNKS - 1) as c:
                    chunk(c, False, rest)
                chunk(CHUNKS - 1, True, rest)

            with pe.If(general):
                dense(True)
            with pe.Else():
                dense(False)


def kernel(x, itok_BxS_13_99985, ctx_2048, L0_ffn_gate_w, L0_ffn_up_w, L0_ffn_down_w,
           L0_ffn_gate_s, L0_ffn_up_s, L0_ffn_down_s):
    import concourse.bacc as bacc
    from concourse.bass_utils import run_bass_kernel_spmd

    x = np.asarray(x)
    shape = x.shape

    def by_slice(w):
        return np.asarray(w).reshape(SLICES, P, KD, P).transpose(0, 3, 2, 1).reshape(SLICES, P, D)

    down = np.asarray(L0_ffn_down_w).T.reshape(SLICES, P, D)
    arrays = {
        "consts": constants(),
        "tok": np.asarray(itok_BxS_13_99985).reshape(P, TILES),
        "x_rows": x.reshape(TOKENS, D),
        "ctx_t": np.asarray(ctx_2048).transpose(0, 2, 1).reshape(EXPERTS, KD, P, D)
                   .transpose(0, 2, 1, 3).reshape(EXPERTS, P, KD * D),
        "ffn_w": np.concatenate([by_slice(L0_ffn_gate_w), by_slice(L0_ffn_up_w), down], axis=2),
        "scales": np.concatenate([np.asarray(L0_ffn_gate_s).reshape(SLICES, P).T,
                                  np.asarray(L0_ffn_up_s).reshape(SLICES, P).T], axis=1),
        "down_s": np.broadcast_to(np.asarray(L0_ffn_down_s)[None, :], (P, D)),
    }
    arrays = {k: np.ascontiguousarray(a) for k, a in arrays.items()}
    nc = bacc.Bacc("TRN2", target_bir_lowering=False, num_devices=1)
    args = [nc.dram_tensor(k, a.shape, mybir.dt.from_np(a.dtype), kind="ExternalInput").ap()
            for k, a in arrays.items()]
    res = nc.dram_tensor("y_rows", (TOKENS, D), F32, kind="ExternalOutput").ap()
    build(nc, *args, res)
    r = run_bass_kernel_spmd(nc, [arrays], core_ids=[0])
    return r.results[0]["y_rows"].reshape(shape)
```
